# Optimizing a Trainium2 kernel written in Bass

```python
import numpy as np
import jax
import jax.numpy as jnp

def _softmax(x, axis=-1):
    return jax.nn.softmax(x, axis=axis)

def _gelu(x):
    return jax.nn.gelu(x, approximate=True)

def _silu(x):
    return jax.nn.silu(x)

def _sigmoid(x):
    return jax.nn.sigmoid(x)

def _layernorm(x, axis=-1, eps=1e-05):
    m = jnp.mean(x, axis=axis, keepdims=True)
    v = jnp.var(x, axis=axis, keepdims=True)
    return (x - m) / jnp.sqrt(v + eps)

def _scatter_add(tgt, idx, src, axis=0):
    return tgt.at[idx].add(src)

def _segment_sum(src, seg, n):
    return jax.ops.segment_sum(src, seg, n)
kernel_name = 'mk_xattn_ffn_d1_seqx_r4_1186a9'

def setup_inputs(seed: int=0):
    np.random.seed(seed)
    _w = jnp.asarray

    def _rec_inputs():
        import jax
        import jax.numpy as jnp
        _rk = jax.random.key(seed)
        x = 7.22e-05 + 1 * jax.random.normal(jax.random.fold_in(_rk, 1), (8, 256, 256), jnp.float32)
        _lenS = 256 - jax.random.randint(jax.random.fold_in(_rk, 7), (8,), 0, max(1, 256 // 4) + 1, jnp.int32)
        _lenS2 = 77 - jax.random.randint(jax.random.fold_in(_rk, 8), (8,), 0, max(1, 77 // 4) + 1, jnp.int32)
        _ctx_1024P = jax.random.normal(jax.random.fold_in(_rk, 11), (8, 16, 256), jnp.float32)
        _ctx_1024c = jax.random.dirichlet(jax.random.fold_in(_rk, 511), 0.3 * jnp.ones((16,), jnp.float32), (8, 77))
        _ctx_1024t = jnp.einsum('bsk,bkd->bsd', _ctx_1024c, _ctx_1024P)
        _ctx_1024t = _ctx_1024t * jax.lax.rsqrt(jnp.mean(jnp.square(_ctx_1024t)) + 1e-12) * 0.953939
        ctx_1024 = 4.13588e-05 + 0.999923 * (_ctx_1024t + 0.3 * jax.random.normal(jax.random.fold_in(_rk, 611), (8, 77, 256), jnp.float32))
        _validS = jnp.arange(256)[None, :] < _lenS[:, None]
        _validS2 = jnp.arange(77)[None, :] < _lenS2[:, None]
        _causal = jnp.tril(jnp.ones((256, 256), dtype=bool))
        mask_BxSxS2_ik1 = jnp.where(jnp.broadcast_to(_validS2[:, None, :], (8, 256, 77)), 1, 0).astype(jnp.int32)
        return (x, ctx_1024, mask_BxSxS2_ik1)
    x, ctx_1024, mask_BxSxS2_ik1 = _rec_inputs()

    def _L0_xattn_setup():
        import jax, jax.numpy as jnp
        import numpy as np
        NEG = -9000000000000000.0
        EPS = 1e-05
        key = jax.random.key(seed)
        k1, k2, k3, k4 = jax.random.split(key, 4)
        B, S, D = (4, 512, 256)
        q = jax.random.normal(k1, (B, S, D), dtype=jnp.float32)
        k = jax.random.normal(k2, (B, S, D), dtype=jnp.float32)
        v = jax.random.normal(k3, (B, S, D), dtype=jnp.float32)
        mask = jax.random.randint(k4, (B, S, S), 0, 2, dtype=jnp.int32)
        gamma = jnp.ones((D,), dtype=jnp.float32)
        beta = jnp.zeros((D,), dtype=jnp.float32)
        return {'q': q, 'k': k, 'v': v, 'mask': mask, 'gamma': gamma, 'beta': beta}
    _L0_xattn_all = _L0_xattn_setup()
    _L0_xattn_in = {k: v for k, v in _L0_xattn_all.items() if k in ('gamma', 'beta')}
    del _L0_xattn_all

    def _L0_ffn_setup():
        import jax, jax.numpy as jnp
        import numpy as np
        B, S, D = (2, 512, 256)
        F = 1024
        E, K = (8, 2)
        EPS = 1e-09
        key = jax.random.key(seed)
        k1, k2, k3, k4 = jax.random.split(key, 4)
        x = jax.random.normal(k1, (B, S, D), dtype=jnp.float32)
        w_gate = jax.random.normal(k2, (D, E), dtype=jnp.float32) * 0.02
        w_gate_up = jax.random.normal(k3, (E, D, 2 * F), dtype=jnp.float32) * 0.02
        w_down = jax.random.normal(k4, (E, F, D), dtype=jnp.float32) * 0.02
        return {'x': x, 'w_gate': w_gate, 'w_gate_up': w_gate_up, 'w_down': w_down}
    _L0_ffn_all = _L0_ffn_setup()
    _L0_ffn_in = {k: v for k, v in _L0_ffn_all.items() if k in ('w_gate', 'w_gate_up', 'w_down')}
    del _L0_ffn_all
    return {'x': x, 'ctx_1024': ctx_1024, 'mask_BxSxS2_ik1': mask_BxSxS2_ik1, 'L0_xattn_gamma': _L0_xattn_in['gamma'], 'L0_xattn_beta': _L0_xattn_in['beta'], 'L0_ffn_w_gate': _L0_ffn_in['w_gate'], 'L0_ffn_w_gate_up': _L0_ffn_in['w_gate_up'], 'L0_ffn_w_down': _L0_ffn_in['w_down']}

def reference(x, ctx_1024, mask_BxSxS2_ik1, L0_xattn_gamma, L0_xattn_beta, L0_ffn_w_gate, L0_ffn_w_gate_up, L0_ffn_w_down):
    import jax
    import jax.numpy as jnp

    def _L0_xattn_ref(q, k, v, mask, gamma, beta):
        import jax, jax.numpy as jnp
        import numpy as np
        NEG = -9000000000000000.0
        EPS = 1e-05
        d_k = q.shape[-1]
        logits = jnp.einsum('bsd,btd->bst', q, k) / jnp.sqrt(jnp.asarray(d_k, q.dtype))
        logits = jnp.where(mask == 0, jnp.asarray(NEG, logits.dtype), logits)
        attn = jax.nn.softmax(logits, axis=-1)
        x = jnp.einsum('bst,btd->bsd', attn, v)
        mu = jnp.mean(x, axis=-1, keepdims=True)
        var = jnp.mean(jnp.square(x - mu), axis=-1, keepdims=True)
        xhat = (x - mu) * jax.lax.rsqrt(var + EPS)
        return xhat * gamma + beta

    def _L0_ffn_ref(x, w_gate, w_gate_up, w_down):
        import jax, jax.numpy as jnp
        import numpy as np
        B, S, D = (2, 512, 256)
        F = 1024
        E, K = (8, 2)
        EPS = 1e-09
        gate_logits = x @ w_gate
        gate_probs = jax.nn.softmax(gate_logits, axis=-1)
        topk_vals, topk_idx = jax.lax.top_k(gate_probs, K)
        masked = jnp.sum(jax.nn.one_hot(topk_idx, E, dtype=gate_probs.dtype) * topk_vals[..., None], axis=-2)
        denom = jnp.maximum(jnp.sum(masked, axis=-1, keepdims=True), EPS)
        gate_probs = masked / denom
        gu = jnp.einsum('bsd,edh->ebsh', x, w_gate_up)
        g, u = jnp.split(gu, 2, axis=-1)
        act = jax.nn.silu(g) * u
        expert_out = jnp.einsum('ebsf,efd->ebsd', act, w_down)
        return jnp.einsum('bse,ebsd->bsd', gate_probs, expert_out)
    x = x + _L0_xattn_ref(_layernorm(x, axis=-1), ctx_1024, ctx_1024, mask_BxSxS2_ik1, L0_xattn_gamma, L0_xattn_beta)
    x = x + _L0_ffn_ref(_layernorm(x, axis=-1), L0_ffn_w_gate, L0_ffn_w_gate_up, L0_ffn_w_down)
    return x

_drawn_inputs = setup_inputs


def setup_inputs(seed=0):
    import zlib

    import numpy as np

    out = dict(_drawn_inputs(seed))
    spreads = {'L0_xattn_gamma': (1.0, 0.2), 'L0_xattn_beta': (0.0, 0.1)}
    factors = {'L0_ffn_w_gate': 4.038, 'L0_ffn_w_gate_up': 3.529, 'L0_ffn_w_down': 3.521}
    for name, (base, spread) in spreads.items():
        noise = np.random.default_rng([zlib.crc32(name.encode()), seed]).standard_normal(out[name].shape)
        drawn = base * np.exp(spread * noise) if base else spread * noise
        out[name] = jnp.asarray(drawn.astype(out[name].dtype))
    for name, factor in factors.items():
        out[name] = (out[name] * factor).astype(out[name].dtype)
    return out
```

```python
from contextlib import ExitStack

import concourse.bass as bass
from concourse import mybir

F32 = mybir.dt.float32
F32R = mybir.dt.float32r
BF16 = mybir.dt.bfloat16
I32 = mybir.dt.int32
ALU = mybir.AluOpType
ACT = mybir.ActivationFunctionType
X = mybir.AxisListType.X
P = 128
NEG = -9e15
NO_CAP = 3e38
EPS = 1e-5
GATE_EPS = 1e-9


def block_count(tokens, experts):
    return (2 * tokens - experts) // P + experts


def build(nc, x, ctx, mask, gamma, beta, w_gate, w_gate_up, w_down, out):
    B, S, D = x.shape
    T = ctx.shape[1]
    E, _, F2 = w_gate_up.shape
    F = F2 // 2
    KD = D // P
    TOK = B * S
    NT = TOK // P
    TPB = S // P
    HB, HT = B // 2, NT // 2
    NBLK = block_count(TOK, E)
    HALF = F // 2
    CH = HALF // P
    ROW = D + 2
    PIECE = 4 * D
    PIECES = (KD * F2 + F // P * D) // PIECE
    GU = KD * F2 // PIECE
    RAW = 3
    QUOTA = 2
    GROUPS = 4
    assert NBLK % 2 == 1 and HALF == 512 and TPB == 2 and KD == 2 and F == PIECE and D == 2 * P

    x_t = x.rearrange("b (j p) d -> p (b j) d", p=P)
    mask_t = mask.rearrange("b (j p) t -> p (b j) t", p=P)
    ctx_t = ctx.rearrange("b t d -> t b d")
    out_t = out[0:TOK, :].rearrange("(n p) d -> p n d", p=P)
    slots = nc.dram_tensor("slots", (NBLK * P, ROW), F32).ap()
    slots_t = slots.rearrange("(n p) c -> p n c", p=P)

    with ExitStack() as stack:
        def sb(name, shape, dt=F32):
            return stack.enter_context(nc.sbuf_tensor(name, shape, dt))

        def sem(name):
            return stack.enter_context(nc.semaphore(name))

        ident = sb("ident", [P, P])
        before = sb("before", [P, P], BF16)
        ones = sb("ones", [P, P], BF16)
        ones_f = sb("ones_f", [P, P])
        up_to = sb("up_to", [P, E, E])
        descend = sb("descend", [P, E])
        block_start = sb("block_start", [1, NBLK])
        neg_half = sb("neg_half", [P, HT])
        gamma_b = sb("gamma_b", [P, D])
        beta_b = sb("beta_b", [P, D])
        empty = sb("empty", [P, ROW])
        x_sb = sb("x_sb", [P, NT, D])
        ctx_sb = sb("ctx_sb", [T, B, D])
        wg_sb = sb("wg_sb", [P, KD, E])
        cap = sb("cap", [P, NT, T])
        ctxT = sb("ctxT", [P, B, KD, T])
        logit = sb("logit", [P, NT, T])
        row_max = sb("row_max", [P, NT])
        row_sum = sb("row_sum", [P, NT])
        rows = sb("rows", [P, NT, ROW])
        act = sb("act", [P, 2, HALF])
        gated = sb("gated", [P, 2, HALF])
        y_sb = sb("y_sb", [P, 2, D])
        q_sb = act[:, :, :].rearrange("p s (j d) -> p s j d", j=TPB)
        qT = gated[:, :, :].rearrange("p s (j c) -> p s j c", j=TPB * KD)
        probsT = y_sb[0:T, :, :].rearrange("p s (j c) -> p s j c", j=TPB)
        stats = sb("stats", [P, 3, NT, 6])
        mv = sb("mv", [P, 3, NT, 2])
        var_eps = sb("var_eps", [P, 3, NT])
        rstd = sb("rstd", [P, 3, NT])
        inv_sum = sb("inv_sum", [P, NT])
        inv_sq = sb("inv_sq", [P, NT])
        var_n = sb("var_n", [P, NT])
        att_scale = sb("att_scale", [P, NT])
        att_bias = sb("att_bias", [P, NT])
        row_bias = sb("row_bias", [P, NT])
        mean_part = sb("mean_part", [P, NT, E])
        centred = sb("centred", [P, NT, E])
        gates = sb("gates", [P, NT, E])
        gmax = sb("gmax", [P, NT])
        gshift = sb("gshift", [P, NT, E])
        gexp = sb("gexp", [P, NT, E])
        gsum = sb("gsum", [P, NT])
        ginv = sb("ginv", [P, NT])
        prob = sb("prob", [P, NT, E])
        best = sb("best", [P, NT])
        tied = sb("tied", [P, NT, E])
        tied_rank = sb("tied_rank", [P, NT, E])
        first = sb("first", [P, NT])
        top1 = sb("top1", [P, NT, E])
        top2 = sb("top2", [P, NT, E])
        chosen = sb("chosen", [P, NT, E], BF16)
        denom = sb("denom", [P, NT])
        denom_g = sb("denom_g", [P, NT])
        dinv = sb("dinv", [P, NT])
        weight = sb("weight", [P, NT, E])
        count_up = sb("count_up", [P, E], I32)
        blocks_i = sb("blocks_i", [P, E], I32)
        padded = sb("padded", [P, E])
        cum_part = sb("cum_part", [P, E, E])
        ends = sb("ends", [P, E])
        starts = sb("starts", [P, E])
        slot_c = sb("slot_c", [P, NT, E])
        last_slot = sb("last_slot", [P, NT])
        both = sb("both", [P, NT])
        first_slot = sb("first_slot", [P, NT])
        w_last = sb("w_last", [P, NT, E])
        idx = sb("idx", [P, 2, NT], I32)
        past = sb("past", [1, NBLK, E - 1])
        past_start = sb("past_start", [1, NBLK, E - 1])
        expert_f = sb("expert_f", [1, NBLK])
        expert_i = sb("expert_i", [1, NBLK], I32)
        began = sb("began", [1, NBLK])
        due = sb("due", [1, 4, NBLK])
        reached = sb("reached", [1, 2, NT])
        tiles_due = sb("tiles_due", [1, 2])
        place_t = sb("place_t", [1, NBLK], I32)
        weights_t = sb("weights_t", [1, NBLK], I32)
        rows_t = sb("rows_t", [1, NBLK], I32)
        group_t = sb("group_t", [1, 2, GROUPS], I32)
        split_t = sb("split_t", [1, NBLK + 1], I32)
        raw = sb("raw", [P, RAW, 4, D])
        w2 = sb("w2", [P, 2 * PIECES, 4, 2, D], F32R)
        tok = sb("tok", [P, 2, ROW])
        tokT_hi = sb("tokT_hi", [P, 2, KD, P], F32R)
        tokT_lo = sb("tokT_lo", [P, 2, KD, P], F32R)
        aT_hi = sb("aT_hi", [P, 2, CH, P], F32R)
        aT_lo = sb("aT_lo", [P, 2, CH, P], F32R)
        y_low = sb("y_low", [P, D])
        y_idx = sb("y_idx", [P, 2], I32)
        keys = sb("keys", [P, NBLK, 2], I32)

        bank = [stack.enter_context(nc.psum_tensor(f"bank{i}", [P, 512], F32)) for i in range(8)]
        ps_qT = [bank[i][:, :].rearrange("p (j c) -> p j c", j=TPB * KD) for i in (0, 1)]
        ps_logit = [bank[i][:, 0:TPB * T].rearrange("p (j t) -> p j t", j=TPB) for i in (2, 3)]
        ps_pT = [bank[i][0:T, 0:TPB * P].rearrange("p (j c) -> p j c", j=TPB) for i in (4, 5)]
        ps_att = [bank[i][:, :].rearrange("p (j d) -> p j d", j=TPB) for i in (6, 7)]
        ps_ctxT = [bank[i][:, 0:2 * KD * T].rearrange("p (b k t) -> p b k t", b=2, k=KD) for i in (2, 3)]
        ps_gate = bank[2][:, 0:NT * E]
        ps_rank = bank[3][:, 0:NT * E]
        ps_count = bank[4][:, 0:E]
        ps_colsum = bank[5][:, 0:E]
        ps_g = [bank[0], bank[2]]
        ps_u = [bank[1], bank[3]]
        ps_aT = [bank[4], bank[5]]
        ps_tokT = bank[6][:, 0:KD * P]
        ps_y = bank[7]

        def grid(ap):
            return ap.rearrange("p (n e) -> p n e", e=E)

        def over_e(ap):
            return ap.unsqueeze(2).to_broadcast([P, NT, E])

        def over_t(ap):
            return ap.unsqueeze(1).to_broadcast([P, NT, E])

        def two(buf, b):
            return buf[:, bass.ds(TPB * b, TPB), :]

        def at(buf, t):
            return buf[:, bass.ds(t, 1), :].rearrange("p a d -> p (a d)")

        def one(buf, t):
            return buf[:, bass.ds(t, 1)]

        x_in = [sem(f"x_in{i}") for i in range(4)]
        mask_in = sem("mask_in")
        ctx_in = sem("ctx_in")
        gamma_in = sem("gamma_in")
        beta_in = sem("beta_in")
        wg_in = sem("wg_in")
        raw_in = sem("raw_in")
        loading = sem("loading")
        const = sem("const")
        zeroed = sem("zeroed")
        empty_set = sem("empty_set")
        spare_out = sem("spare_out")
        slots_empty = sem("slots_empty")
        stats1 = sem("stats1")
        var1 = sem("var1")
        rstd1 = sem("rstd1")
        cap_step = sem("cap_step")
        cap_set = sem("cap_set")
        xb_set = sem("xb_set")
        ctxT_ps = sem("ctxT_ps")
        ctxT_set = sem("ctxT_set")
        q_set = sem("q_set")
        qT_ps = sem("qT_ps")
        qT_set = sem("qT_set")
        logit_ps = sem("logit_ps")
        masked = sem("masked")
        max_set = sem("max_set")
        shifted = sem("shifted")
        probs_set = sem("probs_set")
        sum_set = sem("sum_set")
        pT_ps = sem("pT_ps")
        pT_set = sem("pT_set")
        att_ps = sem("att_ps")
        att_set = sem("att_set")
        stats2 = sem("stats2")
        small2 = sem("small2")
        var2 = sem("var2")
        rstd2 = sem("rstd2")
        scale2 = sem("scale2")
        norm2 = sem("norm2")
        gamma_done = sem("gamma_done")
        x1_set = sem("x1_set")
        x1_out = sem("x1_out")
        stats3 = sem("stats3")
        var3 = sem("var3")
        rstd3 = sem("rstd3")
        row_bias_set = sem("row_bias_set")
        rows_set = sem("rows_set")
        x1T_ps = sem("x1T_ps")
        x1T_set = sem("x1T_set")
        colsum_ps = sem("colsum_ps")
        gate_ps = sem("gate_ps")
        route = sem("route")
        gshift_set = sem("gshift_set")
        gexp_set = sem("gexp_set")
        chosen_set = sem("chosen_set")
        rank_ps = sem("rank_ps")
        first_rows = sem("first_rows")
        last_rows = sem("last_rows")
        first_sent = [sem(f"first_sent{i}") for i in range(GROUPS)]
        last_sent = sem("last_sent")
        tables_set = sem("tables_set")
        rows_seen = sem("rows_seen")
        w_hi = sem("w_hi")
        w_lo = sem("w_lo")
        tok_in = [sem(f"tok_in{i}") for i in range(2)]
        tokT_ps = sem("tokT_ps")
        tokT_hi_set = sem("tokT_hi_set")
        tokT_lo_set = sem("tokT_lo_set")
        gu_ps = sem("gu_ps")
        gated_set = sem("gated_set")
        act_set = sem("act_set")
        aT_ps = sem("aT_ps")
        aT_hi_set = sem("aT_hi_set")
        aT_lo_set = sem("aT_lo_set")
        down_done = sem("down_done")
        y_low_set = sem("y_low_set")
        y_set = sem("y_set")
        idx_set = sem("idx_set")
        keys_set = sem("keys_set")
        adding = sem("adding")
        added = sem("added")

        def arrival(b, s):
            return 8 * (b - s) + 16

        def later(b, n):
            return not isinstance(b, int) or b >= n

        def split_high(eng, c):
            eng.wait_ge(raw_in, 16 * (c + 1))
            eng.activation(w2[:, bass.ds(c % (2 * PIECES), 1), :, 0, :].rearrange("p a g d -> p (a g) d"),
                           raw[:, bass.ds(c % RAW, 1)].rearrange("p a g d -> p (a g) d"), ACT.Copy).then_inc(w_hi, 1)

        def split_low(eng, c):
            eng.wait_ge(w_hi, c + 1)
            piece = w2[:, bass.ds(c % (2 * PIECES), 1)]
            eng.tensor_tensor(piece[:, :, :, 1, :].rearrange("p a g d -> p (a g) d"),
                              raw[:, bass.ds(c % RAW, 1)].rearrange("p a g d -> p (a g) d"),
                              piece[:, :, :, 0, :].rearrange("p a g d -> p (a g) d").bitcast(F32),
                              ALU.subtract).then_inc(w_lo, 1)

        def split_due(eng, b, split):
            lo = eng.value_load(split_t[0:1, bass.ds(b, 1)], min_val=PIECES, max_val=PIECES * E)
            hi = eng.value_load(split_t[0:1, bass.ds(b + 1, 1)], min_val=PIECES, max_val=PIECES * E)
            with eng.If(lo < hi):
                with eng.Fori(lo, hi) as c:
                    split(eng, c)

        assert RAW + HB // 2 + 1 == PIECES
        block = stack.enter_context(nc.Block())

        @block.sync
        def _(sp):
            n = NT // 4
            for i in range(4):
                sp.dma_start(x_sb[:, i * n:(i + 1) * n, :], x_t[:, i * n:(i + 1) * n, :]).then_inc(x_in[i], 16)
                if i == 0:
                    sp.dma_start(ctx_sb[:], ctx_t).then_inc(ctx_in, 16)
                if i == 2:
                    sp.dma_start(cap[:].bitcast(I32), mask_t).then_inc(mask_in, 16)
            sp.dma_start(beta_b[:], beta.partition_broadcast(P)).then_inc(beta_in, 16)
            sp.dma_start(gamma_b[:], gamma.partition_broadcast(P)).then_inc(gamma_in, 16)
            sp.dma_start(wg_sb[:], w_gate.rearrange("(k p) e -> p k e", p=P)).then_inc(wg_in, 16)

            def load_piece(e, i):
                c = PIECES * e + i
                if later(c, 1):
                    sp.wait_ge(raw_in, 16 * c)
                if not isinstance(c, int):
                    sp.sem_inc(loading, 1)
                if later(c, RAW):
                    sp.wait_ge(w_lo, c - RAW + 1)
                if not isinstance(c, int):
                    sp.sem_inc(loading, 1)
                if i < GU:
                    k, half = i // (GU // KD), i % (GU // KD)
                    sp.dma_start(raw[:, i % RAW].rearrange("p g d -> p (g d)"),
                                 w_gate_up[bass.ds(e, 1), k * P:(k + 1) * P, half * PIECE:(half + 1) * PIECE]
                                 .rearrange("a p f -> (a p) f")).then_inc(raw_in, 16)
                else:
                    f = (i - GU) * HALF
                    sp.dma_start(raw[:, i % RAW],
                                 w_down[bass.ds(e, 1), f:f + HALF, :].rearrange("a (g p) d -> p (a g) d", p=P)
                                 ).then_inc(raw_in, 16)

            for i in range(RAW):
                load_piece(0, i)
            sp.wait_ge(empty_set, 1)
            sp.dma_start(slots_t, empty[:].unsqueeze(1).to_broadcast([P, NBLK, ROW])).then_inc(slots_empty, 16)
            sp.dma_start(out[TOK:TOK + P, :], empty[:, 0:D]).then_inc(spare_out, 16)
            for i in range(RAW, PIECES):
                load_piece(0, i)
            with sp.Fori(0, B) as b:
                sp.wait_ge(x1_set, b + 1)
                sp.dma_start(out_t[:, bass.ds(TPB * b, TPB), :], two(x_sb, b)).then_inc(x1_out, 16)
            with sp.Fori(1, E) as e:
                for i in range(PIECES):
                    load_piece(e, i)

        @block.gpsimd
        def _(pool):
            pool.memset(ident[:], 0.0).then_inc(zeroed, 1)
            pool.memset(before[:], 0.0).then_inc(zeroed, 1)
            pool.memset(up_to[:], 1.0).then_inc(zeroed, 1)
            pool.memset(empty[:], 0.0).then_inc(zeroed, 1)
            pool.memset(neg_half[:], -0.5).then_inc(const, 1)
            pool.memset(ones[:], 1.0).then_inc(const, 1)
            pool.memset(ones_f[:], 1.0).then_inc(const, 1)
            pool.wait_ge(zeroed, 4)
            pool.affine_select(out=ident[:], in_=ident[:], compare_op=ALU.not_equal, fill=1.0, base=0,
                               pattern=[[-1, P]], channel_multiplier=1).then_inc(const, 1)
            pool.affine_select(out=before[:], in_=before[:], compare_op=ALU.is_ge, fill=1.0, base=0,
                               pattern=[[-1, P]], channel_multiplier=1).then_inc(const, 1)
            pool.affine_select(out=up_to[:], in_=up_to[:], compare_op=ALU.is_ge, fill=0.0, base=0,
                               pattern=[[1, E], [-1, E]], channel_multiplier=0).then_inc(const, 1)
            pool.iota(descend[:], pattern=[[-1, E]], base=E, channel_multiplier=0,
                      allow_small_or_imprecise_dtypes=True).then_inc(const, 1)
            pool.iota(block_start[:], pattern=[[P, NBLK]], base=0, channel_multiplier=0,
                      allow_small_or_imprecise_dtypes=True).then_inc(const, 1)
            pool.iota(empty[:, D + 1:D + 2].bitcast(I32), pattern=[[0, 1]], base=TOK, channel_multiplier=1).then_inc(empty_set, 1)
            pool.iota(rows[:, :, D + 1:D + 2].bitcast(I32), pattern=[[P, NT], [0, 1]], base=0,
                      channel_multiplier=1).then_inc(const, 1)

            def rsqrt(n, t0, t1, ready, count, done):
                pool.wait_ge(ready, count)
                pool.tensor_tensor(rstd[:, n, t0:t1], var_eps[:, n, t0:t1], neg_half[:, 0:t1 - t0], ALU.pow).then_inc(done, 1)

            pool.wait_ge(const, 9)
            for i in range(4):
                rsqrt(0, i * NT // 4, (i + 1) * NT // 4, var1, i + 1, rstd1)
            with pool.Fori(0, PIECES) as c:
                split_low(pool, c)
            pool.wait_ge(beta_in, 16)
            with pool.Fori(0, B) as b:
                pool.wait_ge(q_set, b + 1)
                pool.tensor_tensor(two(x_sb, b), two(x_sb, b), beta_b[:].unsqueeze(1).to_broadcast([P, TPB, D]),
                                   ALU.add).then_inc(xb_set, 1)
            pool.wait_ge(gamma_in, 16)
            for h in range(2):
                rsqrt(1, h * HT, (h + 1) * HT, var2, h + 1, rstd2)
            with pool.Fori(0, B) as b:
                pool.wait_ge(norm2, b + 1)
                a = two(rows, b)[:, :, 0:D]
                pool.tensor_tensor(a, a, gamma_b[:].unsqueeze(1).to_broadcast([P, TPB, D]), ALU.mult).then_inc(gamma_done, 1)
            for h in range(2):
                rsqrt(2, h * HT, (h + 1) * HT, var3, h + 1, rstd3)

            def send(half, n, done):
                pool.indirect_dma_start(
                    out=slots, out_offset=bass.IndirectOffsetOnAxis(ap=idx[:, half, n:n + 1], axis=0),
                    in_=rows[:, n, :], in_offset=None).then_inc(done, 16)

            pool.wait_ge(slots_empty, 16)
            pool.wait_ge(first_rows, 1)
            for n in range(NT):
                if n % TPB == 0:
                    pool.wait_ge(rows_set, n // TPB + 1)
                send(0, n, first_sent[n * GROUPS // NT])
            pool.wait_ge(last_rows, 1)
            for n in range(NT):
                send(1, n, last_sent)
            pool.wait_ge(x1_out, 16 * B)
            pool.wait_ge(spare_out, 16)

            def add(b, s):
                pool.wait_ge(y_set, b + 1)
                pool.wait_ge(idx_set, b + 1)
                pool.sem_inc(adding, 1)
                pool.indirect_dma_start(
                    out=out, out_offset=bass.IndirectOffsetOnAxis(ap=y_idx[:, s:s + 1], axis=0),
                    in_=y_sb[:, s, :], in_offset=None, compute_op=ALU.add).then_inc(added, 16)
                pool.wait_ge(added, 16 * (b + 1))

            add(0, 0)
            with pool.Fori(0, NBLK // 2) as i:
                add(2 * i + 1, 1)
                add(2 * i + 2, 0)

        @block.vector
        def _(dve):
            def aggregate(n, t0, t1, done, count):
                dve.wait_ge(done, count)
                for t in range(t0, t1):
                    dve.bn_aggr(mv[:, n, t, :], stats[:, n, t, :]).then_inc(done, 1)
                dve.wait_ge(done, count + t1 - t0)

            n = NT // 4
            for i in range(4):
                dve.wait_ge(x_in[i], 16)
                for t in range(i * n, (i + 1) * n):
                    dve.bn_stats(stats[:, 0, t, :], x_sb[:, t, :]).then_inc(stats1, 1)
                aggregate(0, i * n, (i + 1) * n, stats1, (2 * i + 1) * n)
                dve.tensor_scalar(var_eps[:, 0, i * n:(i + 1) * n], mv[:, 0, i * n:(i + 1) * n, 1], EPS, None,
                                  ALU.add).then_inc(var1, 1)
            dve.wait_ge(mask_in, 16)
            dve.tensor_scalar(cap[:], cap[:].bitcast(I32), 0.0, NO_CAP, ALU.not_equal, ALU.mult).then_inc(cap_step, 1)
            dve.wait_ge(cap_step, 1)
            dve.tensor_scalar(cap[:], cap[:], NEG, None, ALU.add).then_inc(cap_set, 1)

            def queries(b, s):
                if later(b, 2):
                    dve.wait_ge(qT_ps, b - 1)
                for j in range(TPB):
                    t = TPB * b + j
                    ins = dve.tensor_scalar(q_sb[:, s, j, :], at(x_sb, t), one(mv[:, 0, :, 0], t), one(rstd[:, 0, :], t),
                                            ALU.subtract, ALU.mult)
                ins.then_inc(q_set, 1)

            def masked_logits(b, s):
                dve.wait_ge(logit_ps, b + 1)
                dve.scalar_tensor_tensor(out=two(logit, b), in0=ps_logit[s], scalar=float(D) ** -0.5,
                                         in1=two(cap, b), op0=ALU.mult, op1=ALU.min).then_inc(masked, 1)

            def shift(h):
                part, top = logit[:, h * HT:(h + 1) * HT, :], row_max[:, h * HT:(h + 1) * HT]
                dve.wait_ge(masked, (h + 1) * HB)
                dve.tensor_reduce(top, part, X, ALU.max).then_inc(max_set, 1)
                dve.wait_ge(max_set, h + 1)
                dve.tensor_tensor(part, part, top.unsqueeze(2).to_broadcast([P, HT, T]), ALU.subtract).then_inc(shifted, 1)

            def queries_and_logits(p):
                for s in range(2):
                    queries(2 * p + 2 + s, s)
                    masked_logits(2 * p + s, s)

            dve.wait_ge(rstd1, 4)
            dve.wait_ge(cap_set, 1)
            for s in range(2):
                queries(s, s)
            with dve.Fori(0, HB // 2) as p:
                queries_and_logits(p)
            shift(0)
            queries_and_logits(HB // 2)
            for s in range(2):
                masked_logits(B - 2 + s, s)
            shift(1)
            for h in range(2):
                dve.wait_ge(probs_set, h + 1)
                dve.tensor_reduce(row_sum[:, h * HT:(h + 1) * HT], logit[:, h * HT:(h + 1) * HT, :], X, ALU.add).then_inc(sum_set, 1)
            dve.wait_ge(sum_set, 2)
            dve.reciprocal(inv_sum[:], row_sum[:]).then_inc(small2, 1)
            dve.wait_ge(small2, 1)
            dve.tensor_tensor(inv_sq[:], inv_sum[:], inv_sum[:], ALU.mult).then_inc(small2, 1)

            def variances(h):
                with dve.Fori(h * HB, (h + 1) * HB) as b:
                    dve.wait_ge(att_set, b + 1)
                    for j in range(TPB):
                        dve.bn_stats(at(stats[:, 1], TPB * b + j), at(rows, TPB * b + j)[:, 0:D]).then_inc(stats2, 1)
                aggregate(1, h * HT, (h + 1) * HT, stats2, (2 * h + 1) * HT)
                part = slice(h * HT, (h + 1) * HT)
                dve.wait_ge(small2, 2)
                dve.tensor_tensor(var_n[:, part], mv[:, 1, part, 1], inv_sq[:, part], ALU.mult).then_inc(small2, 1)
                dve.wait_ge(small2, 3 + h)
                dve.tensor_scalar(var_eps[:, 1, part], var_n[:, part], EPS, None, ALU.add).then_inc(var2, 1)

            def scales(h):
                part = slice(h * HT, (h + 1) * HT)
                dve.wait_ge(rstd2, h + 1)
                dve.tensor_tensor(att_scale[:, part], inv_sum[:, part], rstd[:, 1, part], ALU.mult).then_inc(scale2, 1)
                dve.wait_ge(scale2, 2 * h + 1)
                dve.scalar_tensor_tensor(out=att_bias[:, part], in0=mv[:, 1, part, 0], scalar=-1.0, in1=att_scale[:, part],
                                         op0=ALU.mult, op1=ALU.mult).then_inc(scale2, 1)

            def residual(b):
                dve.wait_ge(gamma_done, b + 1)
                dve.wait_ge(xb_set, b + 1)
                dve.tensor_tensor(two(x_sb, b), two(rows, b)[:, :, 0:D], two(x_sb, b), ALU.add).then_inc(x1_set, 1)
                dve.wait_ge(x1_set, b + 1)
                for j in range(TPB):
                    dve.bn_stats(at(stats[:, 2], TPB * b + j), at(x_sb, TPB * b + j)).then_inc(stats3, 1)

            def x1_variances(h):
                part = slice(h * HT, (h + 1) * HT)
                aggregate(2, h * HT, (h + 1) * HT, stats3, (2 * h + 1) * HT)
                dve.tensor_scalar(var_eps[:, 2, part], mv[:, 2, part, 1], EPS, None, ALU.add).then_inc(var3, 1)

            variances(0)
            scales(0)
            variances(1)
            scales(1)
            with dve.Fori(0, HB) as b:
                residual(b)
            x1_variances(0)
            with dve.Fori(HB, B) as b:
                residual(b)
            x1_variances(1)

            step = [0]

            def then(ins):
                step[0] += 1
                ins.then_inc(route, 1)
                dve.wait_ge(route, step[0])

            dve.wait_ge(colsum_ps, 1)
            dve.wait_ge(stats3, 2 * NT)
            then(dve.tensor_tensor(mean_part[:], over_e(mv[:, 2, :, 0]), over_t(ps_colsum), ALU.mult))
            dve.wait_ge(gate_ps, B)
            then(dve.tensor_tensor(centred[:], grid(ps_gate), mean_part[:], ALU.subtract))
            dve.wait_ge(rstd3, 2)
            dve.scalar_tensor_tensor(out=row_bias[:], in0=mv[:, 2, :, 0], scalar=-1.0, in1=rstd[:, 2, :],
                                     op0=ALU.mult, op1=ALU.mult).then_inc(row_bias_set, 1)
            then(dve.tensor_tensor(gates[:], centred[:], over_e(rstd[:, 2, :]), ALU.mult))
            then(dve.tensor_reduce(gmax[:], gates[:], X, ALU.max))
            dve.tensor_tensor(gshift[:], gates[:], over_e(gmax[:]), ALU.subtract).then_inc(gshift_set, 1)
            dve.wait_ge(gshift_set, 1)

            def take_first(top):
                then(dve.tensor_reduce(first[:], tied_rank[:], X, ALU.max))
                then(dve.tensor_tensor(top, tied_rank[:], over_e(first[:]), ALU.is_equal))

            then(dve.scalar_tensor_tensor(out=tied_rank[:], in0=gshift[:], scalar=0.0, in1=over_t(descend[:]),
                                          op0=ALU.is_equal, op1=ALU.mult))
            take_first(top1[:])
            then(dve.scalar_tensor_tensor(out=gates[:], in0=top1[:], scalar=-NO_CAP, in1=gshift[:], op0=ALU.mult, op1=ALU.add))
            then(dve.tensor_reduce(best[:], gates[:], X, ALU.max))
            then(dve.tensor_tensor(tied[:], gates[:], over_e(best[:]), ALU.is_equal))
            then(dve.tensor_tensor(tied_rank[:], tied[:], over_t(descend[:]), ALU.mult))
            take_first(top2[:])
            dve.tensor_tensor(chosen[:], top1[:], top2[:], ALU.add).then_inc(chosen_set, 1)
            dve.wait_ge(gexp_set, 1)
            then(dve.tensor_reduce(gsum[:], gexp[:], X, ALU.add))
            then(dve.reciprocal(ginv[:], gsum[:]))
            then(dve.tensor_tensor(prob[:], gexp[:], over_e(ginv[:]), ALU.mult))
            dve.wait_ge(chosen_set, 1)
            then(dve.tensor_tensor(prob[:], prob[:], chosen[:], ALU.mult))
            then(dve.tensor_reduce(denom[:], prob[:], X, ALU.add))
            then(dve.tensor_scalar(denom_g[:], denom[:], GATE_EPS, None, ALU.max))
            then(dve.reciprocal(dinv[:], denom_g[:]))
            then(dve.tensor_tensor(weight[:], prob[:], over_e(dinv[:]), ALU.mult))
            dve.wait_ge(rank_ps, 1)
            then(dve.tensor_scalar(count_up[:], ps_count, float(P - 1), None, ALU.add))
            then(dve.tensor_scalar(blocks_i[:], count_up[:], P.bit_length() - 1, None, ALU.arith_shift_right))
            then(dve.tensor_scalar(padded[:], blocks_i[:], float(P), float(P), ALU.mult, ALU.max))
            then(dve.tensor_tensor(cum_part[:], up_to[:], padded[:].unsqueeze(1).to_broadcast([P, E, E]), ALU.mult))
            then(dve.tensor_reduce(ends[:], cum_part[:], X, ALU.add))
            then(dve.tensor_tensor(starts[:], ends[:], padded[:], ALU.subtract))
            then(dve.scalar_tensor_tensor(out=slot_c[:], in0=grid(ps_rank), scalar=1.0, in1=over_t(starts[:]),
                                          op0=ALU.add, op1=ALU.add))
            then(dve.tensor_tensor(slot_c[:], slot_c[:], chosen[:], ALU.mult))
            then(dve.tensor_reduce(last_slot[:], slot_c[:], X, ALU.max))
            then(dve.tensor_reduce(both[:], slot_c[:], X, ALU.add))
            then(dve.tensor_tensor(first_slot[:], both[:], last_slot[:], ALU.subtract))
            then(dve.tensor_scalar(idx[:, 0, :], first_slot[:], -1.0, None, ALU.add))
            then(dve.tensor_tensor(w_last[:], slot_c[:], over_e(last_slot[:]), ALU.is_equal))
            then(dve.tensor_tensor(w_last[:], weight[:], w_last[:], ALU.mult))
            then(dve.tensor_tensor(weight[:], weight[:], w_last[:], ALU.subtract))
            dve.tensor_reduce(rows[:, :, D], weight[:], X, ALU.add).then_inc(first_rows, 1)

            ends_row = ends[0:1, 0:E - 1].unsqueeze(1).to_broadcast([1, NBLK, E - 1])
            start_row = block_start[:].unsqueeze(2).to_broadcast([1, NBLK, E - 1])
            then(dve.tensor_tensor(past[:], start_row, ends_row, ALU.is_ge))
            then(dve.tensor_reduce(expert_f[:], past[:], X, ALU.add))
            then(dve.tensor_copy(expert_i[:], expert_f[:]))
            then(dve.tensor_scalar(expert_i[:], expert_i[:], 1, None, ALU.bitwise_and))
            then(dve.tensor_scalar(place_t[:], expert_i[:], float(PIECES), None, ALU.mult))
            then(dve.tensor_scalar(weights_t[:], expert_f[:], float(PIECES), float(PIECES), ALU.mult, ALU.add))
            then(dve.tensor_scalar(rows_t[:], expert_f[:], 1.0, 16.0 * NT, ALU.min, ALU.mult))
            for b in range(2):
                then(dve.tensor_scalar(reached[:, b, :], grid(ps_rank)[0:1, :, 0], float(P * (b + 1)), None, ALU.is_lt))
                then(dve.tensor_scalar(group_t[:, b, :],
                                       reached[:, b, :].rearrange("p (g n) -> p g n", g=GROUPS)[:, :, 0],
                                       16.0 * NT / GROUPS, None, ALU.mult))
            then(dve.tensor_tensor(past_start[:], past[:], ends_row, ALU.mult))
            then(dve.tensor_reduce(began[:], past_start[:], X, ALU.max))
            then(dve.tensor_tensor(due[:, 0, :], block_start[:], began[:], ALU.subtract))
            then(dve.tensor_scalar(due[:, 0, :], due[:, 0, :], QUOTA / P, float(QUOTA + PIECES), ALU.mult, ALU.add))
            then(dve.tensor_scalar(due[:, 1, :], expert_f[:], float(PIECES), None, ALU.mult))
            then(dve.tensor_tensor(due[:, 0, :], due[:, 0, :], due[:, 1, :], ALU.add))
            then(dve.tensor_scalar(due[:, 2, :], due[:, 1, :], 2.0 * PIECES, float(PIECES * E), ALU.add, ALU.min))
            then(dve.tensor_scalar(due[:, 3, :], due[:, 1, :], float(PIECES), None, ALU.add))
            then(dve.tensor_tensor(due[:, 0, 0:NBLK - 1], due[:, 0, 0:NBLK - 1], due[:, 3, 1:NBLK], ALU.max))
            then(dve.tensor_tensor(split_t[:, 1:NBLK + 1], due[:, 0, :], due[:, 2, :], ALU.min))
            dve.memset(split_t[:, 0:1], PIECES).then_inc(tables_set, 1)
            then(dve.tensor_scalar(idx[:, 1, :], last_slot[:], -1.0, None, ALU.add))
            for g in range(GROUPS):
                dve.wait_ge(first_sent[g], 16 * NT // GROUPS)
            dve.tensor_reduce(rows[:, :, D], w_last[:], X, ALU.add).then_inc(last_rows, 1)

            def take_keys(b, s):
                dve.wait_ge(tok_in[s], arrival(b, s))
                dve.tensor_copy(at(keys, b), tok[:, s, D:D + 2].bitcast(I32)).then_inc(keys_set, 1)

            def tok_low(b, s):
                dve.wait_ge(tokT_hi_set, b + 1)
                dve.tensor_tensor(tokT_lo[:, s], ps_tokT.rearrange("p (k c) -> p k c", k=KD), tokT_hi[:, s].bitcast(F32),
                                  ALU.subtract).then_inc(tokT_lo_set, 1)

            def gate_half(b, h):
                dve.wait_ge(gated_set, 2 * b + h + 1)
                if later(b, 1):
                    dve.wait_ge(aT_ps, 2 * b + h - 1)
                dve.tensor_tensor(act[:, h, :], gated[:, h, :], ps_u[h][:, :], ALU.mult).then_inc(act_set, 1)

            def act_low(b, h):
                dve.wait_ge(aT_hi_set, 2 * b + h + 1)
                dve.tensor_tensor(aT_lo[:, h], ps_aT[h][:, :].rearrange("p (k c) -> p k c", k=CH), aT_hi[:, h].bitcast(F32),
                                  ALU.subtract).then_inc(aT_lo_set, 1)

            def weighted(b, s):
                if later(b, 2):
                    dve.wait_ge(added, 16 * (b - 1))
                dve.wait_ge(keys_set, b + 1)
                dve.tensor_copy(y_idx[:, s:s + 1], at(keys, b)[:, 1:2]).then_inc(idx_set, 1)
                dve.wait_ge(y_low_set, b + 1)
                dve.scalar_tensor_tensor(out=y_sb[:, s, :], in0=ps_y[:, 0:D], scalar=at(keys, b)[:, 0:1].bitcast(F32),
                                         in1=y_low[:], op0=ALU.mult, op1=ALU.add).then_inc(y_set, 1)

            def experts(b, s, last=False):
                gate_half(b, 0)
                act_low(b - 1, 1)
                if not last:
                    take_keys(b + 1, 1 - s)
                    tok_low(b + 1, 1 - s)
                gate_half(b, 1)
                act_low(b, 0)
                weighted(b - 1, 1 - s)
                if not last:
                    split_due(dve, b, split_low)

            take_keys(0, 0)
            tok_low(0, 0)
            gate_half(0, 0)
            take_keys(1, 1)
            tok_low(1, 1)
            gate_half(0, 1)
            act_low(0, 0)
            split_due(dve, 0, split_low)
            experts(1, 1)
            experts(2, 0)
            with dve.Fori(1, NBLK // 2 - 1) as i:
                experts(2 * i + 1, 1)
                experts(2 * i + 2, 0)
            experts(NBLK - 2, 1)
            experts(NBLK - 1, 0, last=True)
            act_low(NBLK - 1, 1)
            weighted(NBLK - 1, 0)

        @block.scalar
        def _(act_e):
            for g in range(B // 2):
                act_e.wait_ge(ctxT_ps, g + 1)
                act_e.activation(ctxT[:, 2 * g:2 * g + 2, :, :], ps_ctxT[g % 2], ACT.Copy).then_inc(ctxT_set, 1)

            def copy_qT(b, s):
                act_e.wait_ge(qT_ps, b + 1)
                if later(b, 2):
                    act_e.wait_ge(logit_ps, b - 1)
                act_e.activation(qT[:, s], ps_qT[s], ACT.Copy).then_inc(qT_set, 1)

            def exps(h):
                act_e.wait_ge(shifted, h + 1)
                part = logit[:, h * HT:(h + 1) * HT, :]
                act_e.activation(part, part, ACT.Exp).then_inc(probs_set, 1)

            with act_e.Fori(0, RAW) as c:
                split_high(act_e, c)
            for s in range(2):
                copy_qT(s, s)
            with act_e.Fori(1, HB // 2 + 1) as p:
                for s in range(2):
                    copy_qT(2 * p + s, s)
                split_high(act_e, p + RAW - 1)
            exps(0)
            for s in range(2):
                copy_qT(B - 2 + s, s)
            exps(1)
            split_high(act_e, RAW + 2)

            def copy_pT(b, s):
                act_e.wait_ge(pT_ps, b + 1)
                act_e.activation(probsT[:, s], ps_pT[s], ACT.Copy).then_inc(pT_set, 1)

            def copy_att(b, s):
                act_e.wait_ge(att_ps, b + 1)
                act_e.activation(two(rows, b)[:, :, 0:D], ps_att[s], ACT.Copy).then_inc(att_set, 1)

            for s in range(2):
                copy_pT(s, s)
            with act_e.Fori(0, B // 2 - 1) as p:
                for s in range(2):
                    copy_att(2 * p + s, s)
                    copy_pT(2 * p + 2 + s, s)
            for s in range(2):
                copy_att(B - 2 + s, s)

            def normed(b):
                for j in range(TPB):
                    a = at(rows, TPB * b + j)[:, 0:D]
                    ins = act_e.activation(a, a, ACT.Identity, bias=one(att_bias[:, :], TPB * b + j),
                                           scale=one(att_scale[:, :], TPB * b + j))
                ins.then_inc(norm2, 1)

            def copy_x1T(b, s):
                act_e.wait_ge(x1T_ps, b + 1)
                if later(b, 2):
                    act_e.wait_ge(gate_ps, b - 1)
                act_e.activation(qT[:, s], ps_qT[s], ACT.Copy).then_inc(x1T_set, 1)

            act_e.wait_ge(scale2, 2)
            for b in range(2):
                normed(b)
            with act_e.Fori(0, HB // 2 - 1) as p:
                for s in range(2):
                    normed(2 * p + 2 + s)
                    copy_x1T(2 * p + s, s)
            act_e.wait_ge(scale2, 4)
            with act_e.Fori(HB // 2 - 1, B // 2 - 1) as p:
                for s in range(2):
                    normed(2 * p + 2 + s)
                    copy_x1T(2 * p + s, s)
            for s in range(2):
                copy_x1T(B - 2 + s, s)
            act_e.wait_ge(gshift_set, 1)
            act_e.activation(gexp[:], gshift[:], ACT.Exp).then_inc(gexp_set, 1)

            act_e.wait_ge(row_bias_set, 1)
            with act_e.Fori(0, B) as b:
                act_e.wait_ge(x1_set, b + 1)
                for j in range(TPB):
                    t = TPB * b + j
                    ins = act_e.activation(at(rows, t)[:, 0:D], at(x_sb, t), ACT.Identity, bias=one(row_bias[:, :], t),
                                           scale=one(rstd[:, 2, :], t))
                ins.then_inc(rows_set, 1)

            act_e.wait_ge(tables_set, 1)

            def wait_unless_zero(of, count):
                with act_e.If(count > 0):
                    act_e.wait_ge(of, count)
                    act_e.sem_inc(rows_seen, 1)

            def load_rows(b, s, first_ones=False):
                if first_ones:
                    sent = [act_e.value_load(group_t[0:1, b, g:g + 1], min_val=0, max_val=16 * NT // GROUPS)
                            for g in range(GROUPS)]
                all_sent = act_e.value_load(rows_t[0:1, bass.ds(b, 1)], min_val=0, max_val=16 * NT)
                if first_ones:
                    for g in range(GROUPS):
                        wait_unless_zero(first_sent[g], sent[g])
                wait_unless_zero(last_sent, all_sent)
                if later(b, 2):
                    act_e.wait_ge(tokT_ps, b - 1)
                    act_e.wait_ge(keys_set, b - 1)
                act_e.dma_start(tok[:, s, :], at(slots_t, b)).then_inc(tok_in[s], 16)

            def tok_high(b, s):
                act_e.wait_ge(tokT_ps, b + 1)
                act_e.activation(tokT_hi[:, s], ps_tokT.rearrange("p (k c) -> p k c", k=KD), ACT.Copy).then_inc(tokT_hi_set, 1)

            def silu(b, h):
                act_e.wait_ge(gu_ps, 2 * b + h + 1)
                if later(b, 1):
                    act_e.wait_ge(act_set, 2 * b + h - 1)
                act_e.activation(gated[:, h, :], ps_g[h][:, :], ACT.Silu).then_inc(gated_set, 1)

            def act_high(b, h):
                act_e.wait_ge(aT_ps, 2 * b + h + 1)
                if later(b, 1):
                    act_e.wait_ge(down_done, 2 * b + h - 1)
                act_e.activation(aT_hi[:, h], ps_aT[h][:, :].rearrange("p (k c) -> p k c", k=CH), ACT.Copy).then_inc(aT_hi_set, 1)

            def low_result(b):
                act_e.wait_ge(down_done, 2 * b + 2)
                if later(b, 1):
                    act_e.wait_ge(y_set, b)
                act_e.activation(y_low[:], ps_y[:, D:2 * D], ACT.Copy, scale=at(keys, b)[:, 0:1].bitcast(F32)).then_inc(y_low_set, 1)

            def experts(b, s, ahead=2):
                silu(b, 0)
                act_high(b - 1, 1)
                if ahead > 0:
                    tok_high(b + 1, 1 - s)
                if ahead > 1:
                    load_rows(b + 3, 1 - s)
                silu(b, 1)
                act_high(b, 0)
                low_result(b - 1)
                if ahead > 0:
                    split_due(act_e, b, split_high)

            load_rows(0, 0, first_ones=True)
            load_rows(1, 1, first_ones=True)
            for g in range(GROUPS):
                act_e.wait_ge(first_sent[g], 16 * NT // GROUPS)
            tok_high(0, 0)
            load_rows(2, 0)
            silu(0, 0)
            tok_high(1, 1)
            load_rows(3, 1)
            silu(0, 1)
            act_high(0, 0)
            split_due(act_e, 0, split_high)
            experts(1, 1)
            experts(2, 0)
            with act_e.Fori(1, NBLK // 2 - 2) as i:
                experts(2 * i + 1, 1)
                experts(2 * i + 2, 0)
            experts(NBLK - 4, 1)
            experts(NBLK - 3, 0, ahead=1)
            experts(NBLK - 2, 1, ahead=1)
            experts(NBLK - 1, 0, ahead=0)
            act_high(NBLK - 1, 1)
            low_result(NBLK - 1)

        @block.tensor
        def _(pe):
            pe.wait_ge(const, 9)
            pe.wait_ge(ctx_in, 16)
            for g in range(B // 2):
                if g >= 2:
                    pe.wait_ge(ctxT_set, g - 1)
                for b in range(2):
                    for k in range(KD):
                        ins = pe.transpose(ps_ctxT[g % 2][:, b, k, :], ctx_sb[:, 2 * g + b, k * P:(k + 1) * P], ident[0:T, 0:T])
                ins.then_inc(ctxT_ps, 1)

            def turn_q(b, s):
                pe.wait_ge(q_set, b + 1)
                if later(b, 2):
                    pe.wait_ge(qT_set, b - 1)
                for j in range(TPB):
                    for k in range(KD):
                        ins = pe.transpose(ps_qT[s][:, KD * j + k, :], q_sb[:, s, j, k * P:(k + 1) * P], ident[:])
                ins.then_inc(qT_ps, 1)

            def logits(b, s):
                pe.wait_ge(qT_set, b + 1)
                if later(b, 2):
                    pe.wait_ge(masked, b - 1)
                for j in range(TPB):
                    for k in range(KD):
                        ins = pe.matmul(ps_logit[s][:, j, :], qT[:, s, KD * j + k, :],
                                        ctxT[:, bass.ds(b, 1), k, :].rearrange("p a t -> p (a t)"),
                                        start=(k == 0), stop=(k == KD - 1))
                ins.then_inc(logit_ps, 1)

            def turn_probs(b, s):
                if later(b, 2):
                    pe.wait_ge(pT_set, b - 1)
                for j in range(TPB):
                    ins = pe.transpose(ps_pT[s][:, j, :], logit[:, TPB * b + j, :], ident[:])
                ins.then_inc(pT_ps, 1)

            def values(b, s):
                pe.wait_ge(pT_set, b + 1)
                if later(b, 2):
                    pe.wait_ge(att_set, b - 1)
                for j in range(TPB):
                    ins = pe.matmul(ps_att[s][:, j, :], probsT[:, s, j, :], at(ctx_sb, b), start=True, stop=True)
                ins.then_inc(att_ps, 1)

            for s in range(2):
                turn_q(s, s)
            pe.wait_ge(ctxT_set, B // 2)
            for s in range(2):
                turn_q(2 + s, s)
                logits(s, s)
            with pe.Fori(1, B // 2 - 1) as p:
                for s in range(2):
                    turn_q(2 * p + 2 + s, s)
                    logits(2 * p + s, s)
            for s in range(2):
                logits(B - 2 + s, s)
            pe.wait_ge(probs_set, 1)
            for b in range(2):
                turn_probs(b, b)
            for b in range(2, B):
                if b == HB:
                    pe.wait_ge(probs_set, 2)
                turn_probs(b, b % 2)
                values(b - 2, b % 2)
            for s in range(2):
                values(B - 2 + s, s)

            pe.wait_ge(wg_in, 16)
            for k in range(KD):
                ins = pe.matmul(ps_colsum, ones_f[:], wg_sb[:, k, :], start=(k == 0), stop=(k == KD - 1))
            ins.then_inc(colsum_ps, 1)

            def turn_x1(b, s):
                pe.wait_ge(x1_set, b + 1)
                if b >= 2:
                    pe.wait_ge(x1T_set, b - 1)
                for j in range(TPB):
                    for k in range(KD):
                        ins = pe.transpose(ps_qT[s][:, KD * j + k, :], x_sb[:, TPB * b + j, k * P:(k + 1) * P], ident[:])
                ins.then_inc(x1T_ps, 1)

            def gate_logits(b, s):
                pe.wait_ge(x1T_set, b + 1)
                for j in range(TPB):
                    for k in range(KD):
                        ins = pe.matmul(ps_gate[:, E * (TPB * b + j):E * (TPB * b + j + 1)], qT[:, s, KD * j + k, :],
                                        wg_sb[:, k, :], start=(k == 0), stop=(k == KD - 1))
                ins.then_inc(gate_ps, 1)

            turn_x1(0, 0)
            for b in range(1, B):
                turn_x1(b, b % 2)
                gate_logits(b - 1, 1 - b % 2)
            gate_logits(B - 1, (B - 1) % 2)

            pe.wait_ge(chosen_set, 1)
            picks = chosen[:].rearrange("p n e -> p (n e)")
            for t in range(NT):
                pe.matmul(ps_count, ones[:], picks[:, E * t:E * (t + 1)], start=(t == 0), stop=(t == NT - 1))
            pe.matmul(ps_rank, before[:], picks, start=True, stop=False)
            for d in range(1, NT):
                ins = pe.matmul(ps_rank[:, E * d:], ones[:], picks[:, 0:E * (NT - d)], start=False, stop=(d == NT - 1))
            ins.then_inc(rank_ps, 1)

            def turn_tok(b, s):
                pe.wait_ge(tok_in[s], arrival(b, s))
                if later(b, 1):
                    pe.wait_ge(tokT_lo_set, b)
                for k in range(KD):
                    ins = pe.transpose(ps_tokT[:, k * P:(k + 1) * P], tok[:, s, k * P:(k + 1) * P], ident[:])
                ins.then_inc(tokT_ps, 1)

            def gate_up(b, s, h, place):
                if h == 0:
                    pe.wait_ge(tokT_lo_set, b + 1)
                if later(b, 1):
                    pe.wait_ge(act_set, 2 * b + h - 1)
                for k in range(KD):
                    for tokens, part in ((tokT_hi, 0), (tokT_hi, 1), (tokT_lo, 0)):
                        for half, ps in ((0, ps_g[h]), (1, ps_u[h])):
                            w = w2[:, bass.ds(place + k * (GU // KD) + half, 1), 2 * h:2 * h + 2, part, :]
                            ins = pe.matmul(ps[:, :], tokens[:, s, k, :], w.rearrange("p a g d -> p (a g) d"),
                                            start=(k == 0 and tokens is tokT_hi and part == 0),
                                            stop=(k == KD - 1 and tokens is tokT_lo))
                ins.then_inc(gu_ps, 1)

            def turn_act(b, h):
                pe.wait_ge(act_set, 2 * b + h + 1)
                if later(b, 1):
                    pe.wait_ge(aT_lo_set, 2 * b + h - 1)
                for c in range(CH):
                    ins = pe.transpose(ps_aT[h][:, c * P:(c + 1) * P], act[:, h, c * P:(c + 1) * P], ident[:])
                ins.then_inc(aT_ps, 1)

            def down(b, h, place):
                pe.wait_ge(aT_lo_set, 2 * b + h + 1)
                if h == 0 and later(b, 1):
                    pe.wait_ge(y_set, b)
                for c in range(CH):
                    w = w2[:, bass.ds(place + GU + h, 1), c, :, :]
                    pe.matmul(ps_y[:, :], aT_hi[:, h, c, :], w.rearrange("p a t d -> p (a t d)"),
                              start=(h == 0 and c == 0), stop=False, skip_group_check=True)
                    ins = pe.matmul(ps_y[:, 0:D], aT_lo[:, h, c, :], w[:, :, 0, :].rearrange("p a d -> p (a d)"),
                                    start=False, stop=(h == 1 and c == CH - 1), skip_group_check=True)
                ins.then_inc(down_done, 1)

            def place_of(b):
                return pe.value_load(place_t[0:1, bass.ds(b, 1)], min_val=0, max_val=PIECES)

            def weights_there(b):
                pe.wait_ge(w_lo, pe.value_load(weights_t[0:1, bass.ds(b, 1)], min_val=PIECES, max_val=PIECES * E))

            def experts(b, s, last=False):
                place, place_before = place_of(b), place_of(b - 1)
                weights_there(b)
                gate_up(b, s, 0, place)
                turn_act(b - 1, 1)
                down(b - 1, 0, place_before)
                if not last:
                    turn_tok(b + 1, 1 - s)
                gate_up(b, s, 1, place)
                turn_act(b, 0)
                down(b - 1, 1, place_before)

            pe.wait_ge(tables_set, 1)
            turn_tok(0, 0)
            place = place_of(0)
            weights_there(0)
            gate_up(0, 0, 0, place)
            turn_tok(1, 1)
            gate_up(0, 0, 1, place)
            turn_act(0, 0)
            with pe.Fori(0, NBLK // 2 - 1) as i:
                experts(2 * i + 1, 1)
                experts(2 * i + 2, 0)
            experts(NBLK - 2, 1)
            experts(NBLK - 1, 0, last=True)
            turn_act(NBLK - 1, 1)
            place = place_of(NBLK - 1)
            down(NBLK - 1, 0, place)
            down(NBLK - 1, 1, place)


_INS = ["x", "ctx_1024", "mask_BxSxS2_ik1", "L0_xattn_gamma", "L0_xattn_beta", "L0_ffn_w_gate", "L0_ffn_w_gate_up",
        "L0_ffn_w_down"]


def kernel(**inputs):
    import numpy as np
    import concourse.bacc as bacc
    from concourse.bass_utils import run_bass_kernel_spmd as run

    nc = bacc.Bacc("TRN2", target_bir_lowering=False, num_devices=1)
    arrays, args = {}, []
    for name in _INS:
        a = np.ascontiguousarray(inputs[name])
        arrays[f"in_{name}"] = a
        args.append(nc.dram_tensor(f"in_{name}", a.shape, mybir.dt.from_np(a.dtype), kind="ExternalInput").ap())
    B, S, D = inputs["x"].shape
    out = nc.dram_tensor("out", (B * S + P, D), F32, kind="ExternalOutput").ap()
    build(nc, *args, out)
    result = run(nc, [arrays], core_ids=[0])
    return result.results[0]["out"][0:B * S].reshape(B, S, D)
```

```python
from contextlib import ExitStack

import concourse.bass as bass
from concourse import mybir

F32 = mybir.dt.float32
F32R = mybir.dt.float32r
BF16 = mybir.dt.bfloat16
I32 = mybir.dt.int32
ALU = mybir.AluOpType
ACT = mybir.ActivationFunctionType
X = mybir.AxisListType.X
P = 128
NEG = -9e15
NO_CAP = 3e38
EPS = 1e-5
GATE_EPS = 1e-9


def block_count(tokens, experts):
    return (2 * tokens - experts) // P + experts


def build(nc, x, ctx, mask, gamma, beta, w_gate, w_gate_up, w_down, out):
    B, S, D = x.shape
    T = ctx.shape[1]
    E, _, F2 = w_gate_up.shape
    F = F2 // 2
    KD = D // P
    TOK = B * S
    NT = TOK // P
    TPB = S // P
    HB, HT = B // 2, NT // 2
    NBLK = block_count(TOK, E)
    HALF = F // 2
    CH = HALF // P
    ROW = D + 2
    DE, TE = D + E, T + E
    PIECE = 4 * D
    PIECES = (KD * F2 + F // P * D) // PIECE
    GU = KD * F2 // PIECE
    RAW = 3
    QUOTA = 2
    GROUPS = 8
    assert NBLK % 2 == 1 and HALF == 512 and TPB == 2 and KD == 2 and F == PIECE and D == 2 * P

    x_t = x.rearrange("b (j p) d -> p (b j) d", p=P)
    mask_t = mask.rearrange("b (j p) t -> p (b j) t", p=P)
    ctx_t = ctx.rearrange("b t d -> t b d")
    out_t = out[0:TOK, :].rearrange("(n p) d -> p n d", p=P)
    slots = nc.dram_tensor("slots", (NBLK * P, ROW), F32).ap()
    slots_t = slots.rearrange("(n p) c -> p n c", p=P)

    with ExitStack() as stack:
        def sb(name, shape, dt=F32):
            return stack.enter_context(nc.sbuf_tensor(name, shape, dt))

        def sem(name):
            return stack.enter_context(nc.semaphore(name))

        ident = sb("ident", [P, P])
        before = sb("before", [P, P], BF16)
        ones = sb("ones", [P, P], BF16)
        ones_f = sb("ones_f", [P, P])
        up_to = sb("up_to", [P, E, E])
        descend = sb("descend", [P, E])
        block_start = sb("block_start", [1, NBLK])
        neg_half = sb("neg_half", [P, NT])
        gamma_b = sb("gamma_b", [P, D])
        beta_b = sb("beta_b", [P, D])
        empty = sb("empty", [P, ROW])
        x_sb = sb("x_sb", [P, NT, D])
        ctx_sb = sb("ctx_sb", [T, B, DE])
        wg_sb = sb("wg_sb", [P, KD, 3, E])
        gamma_c = sb("gamma_c", [P, KD])
        beta_c = sb("beta_c", [P, KD])
        cap = sb("cap", [P, NT, T])
        ctxT = sb("ctxT", [P, B, KD, TE])
        logit = sb("logit", [P, NT, T])
        row_max = sb("row_max", [P, NT])
        row_sum = sb("row_sum", [P, NT])
        rows = sb("rows", [P, NT, DE])
        act = sb("act", [P, 2, HALF])
        gated = sb("gated", [P, 2, HALF])
        y_sb = sb("y_sb", [P, 2, D])
        q_sb = act[:, :, :].rearrange("p s (j d) -> p s j d", j=TPB)
        qT = gated[:, :, :].rearrange("p s (j c) -> p s j c", j=TPB * KD)
        probsT = y_sb[0:T, :, :].rearrange("p s (j c) -> p s j c", j=TPB)
        stats = sb("stats", [P, 3, NT, 6])
        mv = sb("mv", [P, 3, NT, 2])
        var_eps = sb("var_eps", [P, 3, NT])
        rstd = sb("rstd", [P, 3, NT])
        inv_sum = sb("inv_sum", [P, NT])
        inv_sq = sb("inv_sq", [P, NT])
        var_n = sb("var_n", [P, NT])
        att_scale = sb("att_scale", [P, NT])
        att_bias = sb("att_bias", [P, NT])
        row_bias = sb("row_bias", [P, NT])
        sums = sb("sums", [P, 3, E])
        std1 = sb("std1", [P, NT])
        x_logits = sb("x_logits", [P, NT, E])
        x1_logits = sb("x1_logits", [P, NT, E])
        mean_part = sb("mean_part", [P, NT, E])
        centred = sb("centred", [P, NT, E])
        gates = sb("gates", [P, NT, E])
        gmax = sb("gmax", [P, NT])
        gshift = sb("gshift", [P, NT, E])
        gexp = sb("gexp", [P, NT, E])
        gsum = sb("gsum", [P, NT])
        ginv = sb("ginv", [P, NT])
        prob = sb("prob", [P, NT, E])
        best = sb("best", [P, NT])
        tied = sb("tied", [P, NT, E])
        tied_rank = sb("tied_rank", [P, NT, E])
        first = sb("first", [P, NT])
        top1 = sb("top1", [P, NT, E])
        top2 = sb("top2", [P, NT, E])
        chosen = sb("chosen", [P, NT, E], BF16)
        denom = sb("denom", [P, NT])
        denom_g = sb("denom_g", [P, NT])
        dinv = sb("dinv", [P, NT])
        weight = sb("weight", [P, NT, E])
        count_up = sb("count_up", [P, E], I32)
        blocks_i = sb("blocks_i", [P, E], I32)
        padded = sb("padded", [P, E])
        cum_part = sb("cum_part", [P, E, E])
        ends = sb("ends", [P, E])
        starts = sb("starts", [P, E])
        slot_c = sb("slot_c", [P, NT, E])
        last_slot = sb("last_slot", [P, NT])
        both = sb("both", [P, NT])
        w_first = sb("w_first", [P, NT, E])
        w_last = sb("w_last", [P, NT, E])
        idx = sb("idx", [P, 2, NT], I32)
        past = sb("past", [1, NBLK, E - 1])
        past_start = sb("past_start", [1, NBLK, E - 1])
        expert_f = sb("expert_f", [1, NBLK])
        expert_i = sb("expert_i", [1, NBLK], I32)
        began = sb("began", [1, NBLK])
        due = sb("due", [1, 4, NBLK])
        reached = sb("reached", [1, NT])
        place_t = sb("place_t", [1, NBLK], I32)
        weights_t = sb("weights_t", [1, NBLK], I32)
        rows_t = sb("rows_t", [1, NBLK], I32)
        groups_f = sb("groups_f", [1, 1])
        groups_t = sb("groups_t", [1, 1], I32)
        split_t = sb("split_t", [1, NBLK + 1], I32)
        raw = sb("raw", [P, RAW, 4, D])
        w2 = sb("w2", [P, 2 * PIECES, 4, 2, D], F32R)
        spent = ctxT[:, :, :, :].rearrange("p b k t -> p (b k t)")
        tok = spent[:, 0:2 * ROW].rearrange("p (s c) -> p s c", s=2)
        y_low = spent[:, 2 * ROW:2 * ROW + D]
        shares = spent[:, 2 * ROW + D:2 * ROW + D + 2 * NT * E].rearrange("p (i n e) -> p i n e", i=2, e=E)
        keys = logit[:, :, :].rearrange("p n t -> p (n t)")[:, 0:2 * NBLK].rearrange("p (n c) -> p n c", c=2).bitcast(I32)
        tokT_hi = sb("tokT_hi", [P, 2, KD, P], F32R)
        tokT_lo = sb("tokT_lo", [P, 2, KD, P], F32R)
        aT_hi = sb("aT_hi", [P, 2, CH, P], F32R)
        aT_lo = sb("aT_lo", [P, 2, CH, P], F32R)
        y_idx = sb("y_idx", [P, 2], I32)

        bank = [stack.enter_context(nc.psum_tensor(f"bank{i}", [P, 512], F32)) for i in range(8)]
        ps_qT = [bank[i][:, :].rearrange("p (j c) -> p j c", j=TPB * KD) for i in (0, 1)]
        ps_logit = [bank[i][:, 0:TPB * TE].rearrange("p (j t) -> p j t", j=TPB) for i in (2, 3)]
        ps_pT = [bank[i][0:T, 0:TPB * P].rearrange("p (j c) -> p j c", j=TPB) for i in (4, 5)]
        ps_att = [bank[i][:, 0:DE] for i in (6, 7)]
        ps_ctxT = [bank[i][:, 0:2 * KD * T].rearrange("p (b k t) -> p b k t", b=2, k=KD) for i in (2, 3)]
        ps_rank = bank[3][:, 0:NT * E]
        ps_count = bank[4][:, 0:E]
        ps_ctxg = bank[4][0:T, 0:B * E].rearrange("p (b e) -> p b e", e=E)
        ps_sums = bank[5][:, 0:3 * E]
        ps_g = [bank[0], bank[2]]
        ps_u = [bank[1], bank[3]]
        ps_aT = [bank[4], bank[5]]
        ps_tokT = bank[6][:, 0:KD * P]
        ps_y = bank[7]

        def grid(ap):
            return ap.rearrange("p (n e) -> p n e", e=E)

        def over_e(ap):
            return ap.unsqueeze(2).to_broadcast([P, NT, E])

        def over_t(ap):
            return ap.unsqueeze(1).to_broadcast([P, NT, E])

        def two(buf, b):
            return buf[:, bass.ds(TPB * b, TPB), :]

        def at(buf, t):
            return buf[:, bass.ds(t, 1), :].rearrange("p a d -> p (a d)")

        def one(buf, t):
            return buf[:, bass.ds(t, 1)]

        x_in = [sem(f"x_in{i}") for i in range(4)]
        mask_in = sem("mask_in")
        ctx_in = sem("ctx_in")
        gamma_in = sem("gamma_in")
        beta_in = sem("beta_in")
        wg_in = sem("wg_in")
        raw_in = sem("raw_in")
        loading = sem("loading")
        const = sem("const")
        zeroed = sem("zeroed")
        empty_set = sem("empty_set")
        spare_out = sem("spare_out")
        slots_empty = sem("slots_empty")
        stats1 = sem("stats1")
        var1 = sem("var1")
        rstd1 = sem("rstd1")
        cols_in = sem("cols_in")
        wg_set = sem("wg_set")
        ctxw_set = sem("ctxw_set")
        ctxg_ps = sem("ctxg_ps")
        ctxg_set = sem("ctxg_set")
        sums_ps = sem("sums_ps")
        sums_set = sem("sums_set")
        x_gates = sem("x_gates")
        x_part = sem("x_part")
        att_part = sem("att_part")
        ids_set = sem("ids_set")
        cap_step = sem("cap_step")
        cap_set = sem("cap_set")
        xb_set = sem("xb_set")
        ctxT_ps = sem("ctxT_ps")
        ctxT_set = sem("ctxT_set")
        q_set = sem("q_set")
        qT_ps = sem("qT_ps")
        qT_set = sem("qT_set")
        logit_ps = sem("logit_ps")
        masked = sem("masked")
        max_set = sem("max_set")
        shifted = sem("shifted")
        probs_set = sem("probs_set")
        sum_set = sem("sum_set")
        inv_set = sem("inv_set")
        pT_ps = sem("pT_ps")
        pT_set = sem("pT_set")
        att_ps = sem("att_ps")
        att_set = sem("att_set")
        stats2 = sem("stats2")
        small2 = sem("small2")
        var2 = sem("var2")
        rstd2 = sem("rstd2")
        scale2 = sem("scale2")
        norm2 = sem("norm2")
        gamma_done = sem("gamma_done")
        x1_set = sem("x1_set")
        x1_out = sem("x1_out")
        stats3 = sem("stats3")
        var3 = sem("var3")
        rstd3 = sem("rstd3")
        row_bias_set = sem("row_bias_set")
        rows_set = sem("rows_set")
        route = sem("route")
        tables = sem("tables")
        last_index = sem("last_index")
        gshift_set = sem("gshift_set")
        gexp_set = sem("gexp_set")
        chosen_set = sem("chosen_set")
        rank_ps = sem("rank_ps")
        first_rows = sem("first_rows")
        last_rows = sem("last_rows")
        first_sent = [sem(f"first_sent{i}") for i in range(GROUPS)]
        last_sent = sem("last_sent")
        tables_set = sem("tables_set")
        rows_seen = sem("rows_seen")
        w_hi = sem("w_hi")
        w_lo = sem("w_lo")
        tok_in = [sem(f"tok_in{i}") for i in range(2)]
        tokT_ps = sem("tokT_ps")
        tokT_hi_set = sem("tokT_hi_set")
        tokT_lo_set = sem("tokT_lo_set")
        gu_ps = sem("gu_ps")
        gated_set = sem("gated_set")
        act_set = sem("act_set")
        aT_ps = sem("aT_ps")
        aT_hi_set = sem("aT_hi_set")
        aT_lo_set = sem("aT_lo_set")
        down_done = sem("down_done")
        y_low_set = sem("y_low_set")
        y_set = sem("y_set")
        idx_set = sem("idx_set")
        keys_set = sem("keys_set")
        adding = sem("adding")
        added = sem("added")

        def arrival(b, s):
            return 8 * (b - s) + 16

        def later(b, n):
            return not isinstance(b, int) or b >= n

        def split_high(eng, c):
            eng.wait_ge(raw_in, 16 * (c + 1))
            eng.activation(w2[:, bass.ds(c % (2 * PIECES), 1), :, 0, :].rearrange("p a g d -> p (a g) d"),
                           raw[:, bass.ds(c % RAW, 1)].rearrange("p a g d -> p (a g) d"), ACT.Copy).then_inc(w_hi, 1)

        def split_low(eng, c):
            eng.wait_ge(w_hi, c + 1)
            piece = w2[:, bass.ds(c % (2 * PIECES), 1)]
            eng.tensor_tensor(piece[:, :, :, 1, :].rearrange("p a g d -> p (a g) d"),
                              raw[:, bass.ds(c % RAW, 1)].rearrange("p a g d -> p (a g) d"),
                              piece[:, :, :, 0, :].rearrange("p a g d -> p (a g) d").bitcast(F32),
                              ALU.subtract).then_inc(w_lo, 1)

        def split_due(eng, b, split):
            lo = eng.value_load(split_t[0:1, bass.ds(b, 1)], min_val=PIECES, max_val=PIECES * E)
            hi = eng.value_load(split_t[0:1, bass.ds(b + 1, 1)], min_val=PIECES, max_val=PIECES * E)
            with eng.If(lo < hi):
                with eng.Fori(lo, hi) as c:
                    split(eng, c)

        assert RAW <= HB
        block = stack.enter_context(nc.Block())

        @block.sync
        def _(sp):
            n = NT // 4
            for i in range(4):
                sp.dma_start(x_sb[:, i * n:(i + 1) * n, :], x_t[:, i * n:(i + 1) * n, :]).then_inc(x_in[i], 16)
                if i == 0:
                    sp.dma_start(ctx_sb[:, :, 0:D], ctx_t).then_inc(ctx_in, 16)
                    sp.dma_start(wg_sb[:, :, 0, :], w_gate.rearrange("(k p) e -> p k e", p=P)).then_inc(wg_in, 16)
                    for k in range(KD):
                        part = slice(k * P, (k + 1) * P)
                        sp.dma_start(gamma_c[:, k:k + 1], gamma[part].unsqueeze(1)).then_inc(cols_in, 16)
                        sp.dma_start(beta_c[:, k:k + 1], beta[part].unsqueeze(1)).then_inc(cols_in, 16)
                if i == 1:
                    sp.dma_start(cap[:].bitcast(I32), mask_t).then_inc(mask_in, 16)
            sp.dma_start(beta_b[:], beta.partition_broadcast(P)).then_inc(beta_in, 16)
            sp.dma_start(gamma_b[:], gamma.partition_broadcast(P)).then_inc(gamma_in, 16)

            def load_piece(e, i):
                c = PIECES * e + i
                if later(c, 1):
                    sp.wait_ge(raw_in, 16 * c)
                if not isinstance(c, int):
                    sp.sem_inc(loading, 1)
                if later(c, RAW):
                    sp.wait_ge(w_lo, c - RAW + 1)
                if not isinstance(c, int):
                    sp.sem_inc(loading, 1)
                if i < GU:
                    k, half = i // (GU // KD), i % (GU // KD)
                    sp.dma_start(raw[:, i % RAW].rearrange("p g d -> p (g d)"),
                                 w_gate_up[bass.ds(e, 1), k * P:(k + 1) * P, half * PIECE:(half + 1) * PIECE]
                                 .rearrange("a p f -> (a p) f")).then_inc(raw_in, 16)
                else:
                    f = (i - GU) * HALF
                    sp.dma_start(raw[:, i % RAW],
                                 w_down[bass.ds(e, 1), f:f + HALF, :].rearrange("a (g p) d -> p (a g) d", p=P)
                                 ).then_inc(raw_in, 16)

            for i in range(PIECES):
                load_piece(0, i)
            sp.wait_ge(empty_set, 1)
            sp.dma_start(slots_t, empty[:].unsqueeze(1).to_broadcast([P, NBLK, ROW])).then_inc(slots_empty, 16)
            sp.dma_start(out[TOK:TOK + P, :], empty[:, 0:D]).then_inc(spare_out, 16)
            with sp.Fori(0, B) as b:
                sp.wait_ge(x1_set, b + 1)
                sp.dma_start(out_t[:, bass.ds(TPB * b, TPB), :], two(x_sb, b)).then_inc(x1_out, 16)
            with sp.Fori(1, E) as e:
                for i in range(PIECES):
                    load_piece(e, i)

        @block.gpsimd
        def _(pool):
            pool.memset(ident[:], 0.0).then_inc(zeroed, 1)
            pool.memset(before[:], 0.0).then_inc(zeroed, 1)
            pool.memset(up_to[:], 1.0).then_inc(zeroed, 1)
            pool.memset(empty[:], 0.0).then_inc(zeroed, 1)
            pool.memset(neg_half[:], -0.5).then_inc(const, 1)
            pool.memset(ones[:], 1.0).then_inc(const, 1)
            pool.memset(ones_f[:], 1.0).then_inc(const, 1)
            pool.wait_ge(zeroed, 4)
            pool.affine_select(out=ident[:], in_=ident[:], compare_op=ALU.not_equal, fill=1.0, base=0,
                               pattern=[[-1, P]], channel_multiplier=1).then_inc(const, 1)
            pool.affine_select(out=before[:], in_=before[:], compare_op=ALU.is_ge, fill=1.0, base=0,
                               pattern=[[-1, P]], channel_multiplier=1).then_inc(const, 1)
            pool.affine_select(out=up_to[:], in_=up_to[:], compare_op=ALU.is_ge, fill=0.0, base=0,
                               pattern=[[1, E], [-1, E]], channel_multiplier=0).then_inc(const, 1)
            pool.iota(descend[:], pattern=[[-1, E]], base=E, channel_multiplier=0,
                      allow_small_or_imprecise_dtypes=True).then_inc(const, 1)
            pool.iota(block_start[:], pattern=[[P, NBLK]], base=0, channel_multiplier=0,
                      allow_small_or_imprecise_dtypes=True).then_inc(const, 1)
            pool.iota(empty[:, D + 1:D + 2].bitcast(I32), pattern=[[0, 1]], base=TOK, channel_multiplier=1).then_inc(empty_set, 1)

            def rsqrt(n, t0, t1, ready, count, done):
                pool.wait_ge(ready, count)
                pool.tensor_tensor(rstd[:, n, t0:t1], var_eps[:, n, t0:t1], neg_half[:, 0:t1 - t0], ALU.pow).then_inc(done, 1)

            pool.wait_ge(const, 8)
            rsqrt(0, 0, NT // 4, var1, 1, rstd1)
            pool.wait_ge(wg_in, 16)
            pool.tensor_copy(ctxT[:, :, :, T:TE], wg_sb[:, :, 0, :].unsqueeze(1).to_broadcast([P, B, KD, E])).then_inc(ctxw_set, 1)
            pool.wait_ge(cols_in, 32 * KD)
            for i, col in ((1, gamma_c), (2, beta_c)):
                pool.tensor_tensor(wg_sb[:, :, i, :], wg_sb[:, :, 0, :], col[:].unsqueeze(2).to_broadcast([P, KD, E]),
                                   ALU.mult).then_inc(wg_set, 1)
            for i in range(1, 4):
                rsqrt(0, i * NT // 4, (i + 1) * NT // 4, var1, i + 1, rstd1)

            def add_beta(b):
                pool.wait_ge(q_set, b + 1)
                pool.tensor_tensor(two(x_sb, b), two(x_sb, b), beta_b[:].unsqueeze(1).to_broadcast([P, TPB, D]),
                                   ALU.add).then_inc(xb_set, 1)

            def times_gamma(b):
                pool.wait_ge(norm2, b + 1)
                a = two(rows, b)[:, :, 0:D]
                pool.tensor_tensor(a, a, gamma_b[:].unsqueeze(1).to_broadcast([P, TPB, D]), ALU.mult).then_inc(gamma_done, 1)

            pool.wait_ge(beta_in, 16)
            with pool.Fori(0, RAW) as i:
                split_low(pool, i)
                add_beta(i)
            for b in range(RAW, B):
                add_beta(b)
            pool.wait_ge(gamma_in, 16)
            rsqrt(1, 0, HT, var2, 1, rstd2)
            for b in range(HB - 1):
                times_gamma(b)
            rsqrt(1, HT, NT, var2, 2, rstd2)
            for b in range(HB - 1, B):
                times_gamma(b)
            pool.wait_ge(att_part, 1)
            pool.iota(rows[:, :, D + 1:D + 2].bitcast(I32), pattern=[[P, NT], [0, 1]], base=0,
                      channel_multiplier=1).then_inc(ids_set, 1)
            rsqrt(2, 0, NT, var3, 1, rstd3)
            with pool.Fori(RAW, PIECES) as i:
                split_low(pool, i)

            def send(half, n, done):
                pool.indirect_dma_start(
                    out=slots, out_offset=bass.IndirectOffsetOnAxis(ap=idx[:, half, n:n + 1], axis=0),
                    in_=rows[:, n, 0:ROW], in_offset=None).then_inc(done, 16)

            pool.wait_ge(slots_empty, 16)
            pool.wait_ge(ids_set, 1)
            pool.wait_ge(first_rows, 1)
            for n in range(NT):
                if n % TPB == 0:
                    pool.wait_ge(rows_set, n // TPB + 1)
                send(0, n, first_sent[n * GROUPS // NT])
            pool.wait_ge(last_index, 1)
            pool.wait_ge(last_rows, 1)
            for n in range(NT):
                send(1, n, last_sent)
            pool.wait_ge(x1_out, 16 * B)
            pool.wait_ge(spare_out, 16)

            def add(b, s):
                pool.wait_ge(y_set, b + 1)
                pool.wait_ge(idx_set, b + 1)
                pool.sem_inc(adding, 1)
                pool.indirect_dma_start(
                    out=out, out_offset=bass.IndirectOffsetOnAxis(ap=y_idx[:, s:s + 1], axis=0),
                    in_=y_sb[:, s, :], in_offset=None, compute_op=ALU.add).then_inc(added, 16)
                pool.wait_ge(added, 16 * (b + 1))

            add(0, 0)
            with pool.Fori(0, NBLK // 2) as i:
                add(2 * i + 1, 1)
                add(2 * i + 2, 0)

        @block.vector
        def _(dve):
            ready2, ready3 = (HT, 3 * HT), (HT, 3 * HT)

            def aggregate(n, t0, t1, done, count):
                dve.wait_ge(done, count)
                for t in range(t0, t1):
                    dve.bn_aggr(mv[:, n, t, :], stats[:, n, t, :]).then_inc(done, 1)
                dve.wait_ge(done, count + t1 - t0)

            def x_stats(i):
                n = NT // 4
                dve.wait_ge(x_in[i], 16)
                for t in range(i * n, (i + 1) * n):
                    dve.bn_stats(stats[:, 0, t, :], x_sb[:, t, :]).then_inc(stats1, 1)
                aggregate(0, i * n, (i + 1) * n, stats1, (2 * i + 1) * n)
                dve.tensor_scalar(var_eps[:, 0, i * n:(i + 1) * n], mv[:, 0, i * n:(i + 1) * n, 1], EPS, None,
                                  ALU.add).then_inc(var1, 1)

            def queries(b):
                dve.wait_ge(rstd1, b * 4 // B + 1)
                if b >= 2:
                    dve.wait_ge(qT_ps, b - 1)
                for j in range(TPB):
                    t = TPB * b + j
                    ins = dve.tensor_scalar(q_sb[:, b % 2, j, :], x_sb[:, t, :], mv[:, 0, t, 0:1], rstd[:, 0, t:t + 1],
                                            ALU.subtract, ALU.mult)
                ins.then_inc(q_set, 1)

            def masked_logits(b):
                dve.wait_ge(logit_ps, b + 1)
                tiles = slice(TPB * b, TPB * (b + 1))
                dve.scalar_tensor_tensor(out=logit[:, tiles, :], in0=ps_logit[b % 2][:, :, 0:T], scalar=float(D) ** -0.5,
                                         in1=cap[:, tiles, :], op0=ALU.mult, op1=ALU.min).then_inc(masked, 1)
                dve.tensor_copy(x_logits[:, tiles, :], ps_logit[b % 2][:, :, T:TE]).then_inc(x_gates, 1)

            def shift(h):
                part, top = logit[:, h * HT:(h + 1) * HT, :], row_max[:, h * HT:(h + 1) * HT]
                dve.wait_ge(masked, (h + 1) * HB)
                dve.tensor_reduce(top, part, X, ALU.max).then_inc(max_set, 1)
                dve.wait_ge(max_set, h + 1)
                dve.tensor_tensor(part, part, top.unsqueeze(2).to_broadcast([P, HT, T]), ALU.subtract).then_inc(shifted, 1)

            def divisors(h):
                part = slice(h * HT, (h + 1) * HT)
                dve.wait_ge(probs_set, h + 1)
                dve.tensor_reduce(row_sum[:, part], logit[:, part, :], X, ALU.add).then_inc(sum_set, 1)
                dve.wait_ge(sum_set, h + 1)
                dve.reciprocal(inv_sum[:, part], row_sum[:, part]).then_inc(inv_set, 1)
                dve.wait_ge(inv_set, 2 * h + 1)
                dve.tensor_tensor(inv_sq[:, part], inv_sum[:, part], inv_sum[:, part], ALU.mult).then_inc(inv_set, 1)

            def att_stats(b):
                for t in range(TPB * b, TPB * (b + 1)):
                    dve.wait_ge(att_set, t + 1)
                    dve.bn_stats(stats[:, 1, t, :], rows[:, t, 0:D]).then_inc(stats2, 1)

            def variances(h):
                aggregate(1, h * HT, (h + 1) * HT, stats2, ready2[h])
                part = slice(h * HT, (h + 1) * HT)
                dve.wait_ge(inv_set, 2 * h + 2)
                dve.tensor_tensor(var_n[:, part], mv[:, 1, part, 1], inv_sq[:, part], ALU.mult).then_inc(small2, 1)
                dve.wait_ge(small2, 1 + h)
                dve.tensor_scalar(var_eps[:, 1, part], var_n[:, part], EPS, None, ALU.add).then_inc(var2, 1)

            def scales(h):
                part = slice(h * HT, (h + 1) * HT)
                dve.wait_ge(rstd2, h + 1)
                dve.tensor_tensor(att_scale[:, part], inv_sum[:, part], rstd[:, 1, part], ALU.mult).then_inc(scale2, 1)
                dve.wait_ge(scale2, 2 * h + 1)
                dve.scalar_tensor_tensor(out=att_bias[:, part], in0=mv[:, 1, part, 0], scalar=-1.0, in1=att_scale[:, part],
                                         op0=ALU.mult, op1=ALU.mult).then_inc(scale2, 1)

            def residual(b):
                dve.wait_ge(gamma_done, b + 1)
                dve.wait_ge(xb_set, b + 1)
                tiles = slice(TPB * b, TPB * (b + 1))
                dve.tensor_tensor(x_sb[:, tiles, :], rows[:, tiles, 0:D], x_sb[:, tiles, :], ALU.add).then_inc(x1_set, 1)

            def x1_stats(b):
                dve.wait_ge(x1_set, b + 1)
                for t in range(TPB * b, TPB * (b + 1)):
                    dve.bn_stats(stats[:, 2, t, :], x_sb[:, t, :]).then_inc(stats3, 1)

            def x1_means(h):
                aggregate(2, h * HT, (h + 1) * HT, stats3, ready3[h])

            def x_share():
                dve.reciprocal(std1[:], rstd[:, 0, :]).then_inc(x_part, 1)
                dve.wait_ge(sums_set, 1)
                dve.tensor_tensor(shares[:, 0], over_e(mv[:, 0, :, 0]), over_t(sums[:, 0, :]), ALU.mult).then_inc(x_part, 1)
                dve.wait_ge(x_part, 2)
                dve.tensor_tensor(shares[:, 0], shares[:, 0], over_t(sums[:, 2, :]), ALU.add).then_inc(x_part, 1)
                dve.wait_ge(x_gates, B)
                dve.tensor_tensor(x_logits[:], x_logits[:], over_e(std1[:]), ALU.mult).then_inc(x_part, 1)
                dve.wait_ge(x_part, 4)
                dve.tensor_tensor(x_logits[:], x_logits[:], shares[:, 0], ALU.add).then_inc(x_part, 1)

            def x1_share():
                dve.wait_ge(scale2, 4)
                dve.wait_ge(x_part, 5)
                dve.tensor_tensor(shares[:, 0], rows[:, :, D:DE], over_e(att_scale[:]), ALU.mult).then_inc(att_part, 1)
                dve.tensor_tensor(shares[:, 1], over_e(att_bias[:]), over_t(sums[:, 1, :]), ALU.mult).then_inc(x_part, 1)
                dve.wait_ge(att_part, 1)
                dve.tensor_tensor(shares[:, 0], shares[:, 0], x_logits[:], ALU.add).then_inc(x_part, 1)
                dve.wait_ge(x_part, 7)
                dve.tensor_tensor(x1_logits[:], shares[:, 0], shares[:, 1], ALU.add).then_inc(x_part, 1)

            x_stats(0)
            queries(0)
            queries(1)
            x_stats(1)
            x_stats(2)
            queries(2)
            dve.wait_ge(mask_in, 16)
            dve.tensor_scalar(cap[:], cap[:].bitcast(I32), 0.0, NO_CAP, ALU.not_equal, ALU.mult).then_inc(cap_step, 1)
            dve.wait_ge(cap_step, 1)
            dve.tensor_scalar(cap[:], cap[:], NEG, None, ALU.add).then_inc(cap_set, 1)
            dve.wait_ge(cap_set, 1)
            queries(3)
            masked_logits(0)
            x_stats(3)
            for b in range(1, HB):
                queries(b + 3)
                masked_logits(b)
            dve.wait_ge(sums_ps, 1)
            dve.tensor_copy(sums[:].rearrange("p i e -> p (i e)"), ps_sums).then_inc(sums_set, 1)
            shift(0)
            queries(HB + 3)
            for b in range(HB, B - 2):
                masked_logits(b)
            divisors(0)
            masked_logits(B - 2)
            att_stats(0)
            masked_logits(B - 1)
            shift(1)
            x_share()
            for b in range(1, HB):
                att_stats(b)
            variances(0)
            divisors(1)
            att_stats(HB)
            scales(0)
            att_stats(HB + 1)
            residual(0)
            att_stats(HB + 2)
            residual(1)
            x1_stats(0)
            att_stats(HB + 3)
            variances(1)
            residual(2)
            x1_stats(1)
            x1_stats(2)
            scales(1)
            x1_share()
            residual(3)
            for b in range(HB, HB + 1):
                residual(b)
                x1_stats(b - 1)
            x1_means(0)
            for b in range(HB + 1, B):
                residual(b)
                x1_stats(b - 1)
            x1_stats(B - 1)
            x1_means(1)
            dve.tensor_scalar(var_eps[:, 2, :], mv[:, 2, :, 1], EPS, None, ALU.add).then_inc(var3, 1)

            done = {route: 0, tables: 0}

            def after(chain, ins=None):
                if ins is None:
                    dve.wait_ge(chain, done[chain])
                else:
                    ins.then_inc(chain, 1)
                    done[chain] += 1

            def step(ins):
                after(route, ins)
                after(route)

            dve.wait_ge(stats3, 2 * NT)
            dve.wait_ge(x_part, 8)
            step(dve.tensor_tensor(mean_part[:], over_e(mv[:, 2, :, 0]), over_t(sums[:, 0, :]), ALU.mult))
            step(dve.tensor_tensor(centred[:], x1_logits[:], mean_part[:], ALU.subtract))
            step(dve.tensor_reduce(gmax[:], centred[:], X, ALU.max))
            step(dve.tensor_tensor(gshift[:], centred[:], over_e(gmax[:]), ALU.subtract))
            step(dve.scalar_tensor_tensor(out=tied_rank[:], in0=gshift[:], scalar=0.0, in1=over_t(descend[:]),
                                          op0=ALU.is_equal, op1=ALU.mult))
            step(dve.tensor_reduce(first[:], tied_rank[:], X, ALU.max))
            step(dve.tensor_tensor(top1[:], tied_rank[:], over_e(first[:]), ALU.is_equal))
            step(dve.scalar_tensor_tensor(out=gates[:], in0=top1[:], scalar=-NO_CAP, in1=gshift[:], op0=ALU.mult, op1=ALU.add))
            step(dve.tensor_reduce(best[:], gates[:], X, ALU.max))
            step(dve.tensor_tensor(tied[:], gates[:], over_e(best[:]), ALU.is_equal))
            step(dve.tensor_tensor(tied_rank[:], tied[:], over_t(descend[:]), ALU.mult))
            dve.wait_ge(rstd3, 1)
            dve.scalar_tensor_tensor(out=row_bias[:], in0=mv[:, 2, :, 0], scalar=-1.0, in1=rstd[:, 2, :],
                                     op0=ALU.mult, op1=ALU.mult).then_inc(row_bias_set, 1)
            step(dve.tensor_reduce(first[:], tied_rank[:], X, ALU.max))
            step(dve.tensor_tensor(top2[:], tied_rank[:], over_e(first[:]), ALU.is_equal))
            dve.tensor_tensor(chosen[:], top1[:], top2[:], ALU.add).then_inc(chosen_set, 1)
            dve.tensor_tensor(gshift[:], gshift[:], over_e(rstd[:, 2, :]), ALU.mult).then_inc(gshift_set, 1)
            dve.wait_ge(chosen_set, 1)
            step(dve.tensor_tensor(tied_rank[:], chosen[:], over_t(descend[:]), ALU.mult))
            step(dve.tensor_reduce(first[:], tied_rank[:], X, ALU.max))
            step(dve.tensor_tensor(tied[:], tied_rank[:], over_e(first[:]), ALU.is_equal))
            dve.wait_ge(gexp_set, 1)
            step(dve.tensor_reduce(gsum[:], gexp[:], X, ALU.add))
            step(dve.reciprocal(ginv[:], gsum[:]))
            step(dve.tensor_tensor(prob[:], gexp[:], over_e(ginv[:]), ALU.mult))
            after(tables, dve.tensor_tensor(prob[:], prob[:], chosen[:], ALU.mult))
            dve.wait_ge(rank_ps, 1)
            after(route, dve.tensor_scalar(count_up[:], ps_count, float(P - 1), None, ALU.add))
            after(tables)
            after(tables, dve.tensor_reduce(denom[:], prob[:], X, ALU.add))
            after(route)
            after(route, dve.tensor_scalar(blocks_i[:], count_up[:], P.bit_length() - 1, None, ALU.arith_shift_right))
            after(tables)
            after(tables, dve.tensor_scalar(denom_g[:], denom[:], GATE_EPS, None, ALU.max))
            after(route)
            after(route, dve.tensor_scalar(padded[:], blocks_i[:], float(P), float(P), ALU.mult, ALU.max))
            after(tables)
            after(tables, dve.reciprocal(dinv[:], denom_g[:]))
            after(route)
            after(route, dve.tensor_tensor(cum_part[:], up_to[:], padded[:].unsqueeze(1).to_broadcast([P, E, E]), ALU.mult))
            after(tables)
            after(tables, dve.tensor_tensor(weight[:], prob[:], over_e(dinv[:]), ALU.mult))
            after(route)
            after(route, dve.tensor_reduce(ends[:], cum_part[:], X, ALU.add))
            after(tables)
            after(tables, dve.tensor_tensor(w_first[:], weight[:], tied[:], ALU.mult))
            after(route)
            after(route, dve.tensor_tensor(starts[:], ends[:], padded[:], ALU.subtract))
            after(tables)
            after(tables, dve.tensor_tensor(w_last[:], weight[:], w_first[:], ALU.subtract))
            after(route)
            step(dve.scalar_tensor_tensor(out=slot_c[:], in0=grid(ps_rank), scalar=1.0, in1=over_t(starts[:]),
                                          op0=ALU.add, op1=ALU.add))
            after(route, dve.tensor_tensor(slot_c[:], slot_c[:], chosen[:], ALU.mult))
            dve.wait_ge(ids_set, 1)
            after(tables, dve.tensor_reduce(rows[:, :, D], w_first[:], X, ALU.add))
            after(route)
            after(route, dve.tensor_reduce(last_slot[:], slot_c[:], X, ALU.max))
            step(dve.tensor_reduce(both[:], slot_c[:], X, ALU.add))
            after(tables)
            dve.scalar_tensor_tensor(out=idx[:, 0, :], in0=both[:], scalar=-1.0, in1=last_slot[:],
                                     op0=ALU.add, op1=ALU.subtract).then_inc(first_rows, 1)
            dve.tensor_scalar(idx[:, 1, :], last_slot[:], -1.0, None, ALU.add).then_inc(last_index, 1)

            ends_row = ends[0:1, 0:E - 1].unsqueeze(1).to_broadcast([1, NBLK, E - 1])
            start_row = block_start[:].unsqueeze(2).to_broadcast([1, NBLK, E - 1])
            step(dve.tensor_tensor(past[:], start_row, ends_row, ALU.is_ge))
            after(route, dve.tensor_reduce(expert_f[:], past[:], X, ALU.add))
            after(tables, dve.tensor_tensor(past_start[:], past[:], ends_row, ALU.mult))
            after(route)
            after(route, dve.tensor_copy(expert_i[:], expert_f[:]))
            after(tables)
            after(tables, dve.tensor_reduce(began[:], past_start[:], X, ALU.max))
            after(route)
            after(route, dve.tensor_scalar(expert_i[:], expert_i[:], 1, None, ALU.bitwise_and))
            after(tables)
            after(tables, dve.tensor_tensor(due[:, 0, :], block_start[:], began[:], ALU.subtract))
            after(route)
            after(route, dve.tensor_scalar(place_t[:], expert_i[:], float(PIECES), None, ALU.mult))
            after(tables)
            after(tables, dve.tensor_scalar(due[:, 0, :], due[:, 0, :], QUOTA / P, float(QUOTA + PIECES), ALU.mult, ALU.add))
            after(route, dve.tensor_scalar(weights_t[:], expert_f[:], float(PIECES), float(PIECES), ALU.mult, ALU.add))
            after(route, dve.tensor_scalar(rows_t[:], expert_f[:], 1.0, 16.0 * NT, ALU.min, ALU.mult))
            after(route, dve.tensor_scalar(due[:, 1, :], expert_f[:], float(PIECES), None, ALU.mult))
            after(route, dve.tensor_scalar(reached[:], grid(ps_rank)[0:1, :, 0], float(P), None, ALU.is_lt))
            after(route)
            after(tables)
            after(tables, dve.tensor_tensor(due[:, 0, :], due[:, 0, :], due[:, 1, :], ALU.add))
            after(route, dve.tensor_scalar(due[:, 2, :], due[:, 1, :], 2.0 * PIECES, float(PIECES * E), ALU.add, ALU.min))
            after(route, dve.tensor_scalar(due[:, 3, :], due[:, 1, :], float(PIECES), None, ALU.add))
            after(route, dve.tensor_reduce(groups_f[:], reached[:].rearrange("p (g n) -> p g n", g=GROUPS)[:, :, 0], X, ALU.add))
            after(route)
            after(tables)
            after(tables, dve.tensor_tensor(due[:, 0, 0:NBLK - 1], due[:, 0, 0:NBLK - 1], due[:, 3, 1:NBLK], ALU.max))
            after(tables)
            after(tables, dve.tensor_tensor(split_t[:, 1:NBLK + 1], due[:, 0, :], due[:, 2, :], ALU.min))
            after(route, dve.tensor_copy(groups_t[:], groups_f[:]))
            after(route)
            after(tables)
            dve.memset(split_t[:, 0:1], PIECES).then_inc(tables_set, 1)

            def higher_weights():
                for g in range(GROUPS):
                    dve.wait_ge(first_sent[g], 16 * NT // GROUPS)
                dve.tensor_reduce(rows[:, :, D], w_last[:], X, ALU.add).then_inc(last_rows, 1)

            def take_keys(b, s):
                dve.wait_ge(tok_in[s], arrival(b, s))
                dve.tensor_copy(at(keys, b), tok[:, s, D:D + 2].bitcast(I32)).then_inc(keys_set, 1)

            def tok_low(b, s):
                dve.wait_ge(tokT_hi_set, b + 1)
                dve.tensor_tensor(tokT_lo[:, s], ps_tokT.rearrange("p (k c) -> p k c", k=KD), tokT_hi[:, s].bitcast(F32),
                                  ALU.subtract).then_inc(tokT_lo_set, 1)

            def gate_half(b, h):
                dve.wait_ge(gated_set, 2 * b + h + 1)
                if later(b, 1):
                    dve.wait_ge(aT_ps, 2 * b + h - 1)
                dve.tensor_tensor(act[:, h, :], gated[:, h, :], ps_u[h][:, :], ALU.mult).then_inc(act_set, 1)

            def act_low(b, h):
                dve.wait_ge(aT_hi_set, 2 * b + h + 1)
                dve.tensor_tensor(aT_lo[:, h], ps_aT[h][:, :].rearrange("p (k c) -> p k c", k=CH), aT_hi[:, h].bitcast(F32),
                                  ALU.subtract).then_inc(aT_lo_set, 1)

            def weighted(b, s):
                if later(b, 2):
                    dve.wait_ge(added, 16 * (b - 1))
                dve.wait_ge(keys_set, b + 1)
                dve.tensor_copy(y_idx[:, s:s + 1], at(keys, b)[:, 1:2]).then_inc(idx_set, 1)
                dve.wait_ge(y_low_set, b + 1)
                dve.scalar_tensor_tensor(out=y_sb[:, s, :], in0=ps_y[:, 0:D], scalar=at(keys, b)[:, 0:1].bitcast(F32),
                                         in1=y_low, op0=ALU.mult, op1=ALU.add).then_inc(y_set, 1)

            def experts(b, s, last=False):
                gate_half(b, 0)
                act_low(b - 1, 1)
                if not last:
                    take_keys(b + 1, 1 - s)
                    tok_low(b + 1, 1 - s)
                gate_half(b, 1)
                act_low(b, 0)
                weighted(b - 1, 1 - s)
                if not last:
                    split_due(dve, b, split_low)

            take_keys(0, 0)
            tok_low(0, 0)
            gate_half(0, 0)
            gate_half(0, 1)
            higher_weights()
            act_low(0, 0)
            take_keys(1, 1)
            tok_low(1, 1)
            split_due(dve, 0, split_low)
            experts(1, 1)
            experts(2, 0)
            with dve.Fori(1, NBLK // 2 - 1) as i:
                experts(2 * i + 1, 1)
                experts(2 * i + 2, 0)
            experts(NBLK - 2, 1)
            experts(NBLK - 1, 0, last=True)
            act_low(NBLK - 1, 1)
            weighted(NBLK - 1, 0)

        @block.scalar
        def _(act_e):
            for g in range(B // 2):
                act_e.wait_ge(ctxT_ps, g + 1)
                act_e.activation(ctxT[:, 2 * g:2 * g + 2, :, 0:T], ps_ctxT[g % 2], ACT.Copy).then_inc(ctxT_set, 1)

            def copy_qT(b):
                act_e.wait_ge(qT_ps, b + 1)
                if b >= 2:
                    act_e.wait_ge(logit_ps, b - 1)
                act_e.activation(qT[:, b % 2], ps_qT[b % 2], ACT.Copy).then_inc(qT_set, 1)

            def exps(h):
                act_e.wait_ge(shifted, h + 1)
                part = logit[:, h * HT:(h + 1) * HT, :]
                act_e.activation(part, part, ACT.Exp).then_inc(probs_set, 1)

            def copy_pT(b):
                act_e.wait_ge(pT_ps, b + 1)
                act_e.activation(probsT[:, b % 2], ps_pT[b % 2], ACT.Copy).then_inc(pT_set, 1)

            def copy_att(b):
                for j in range(TPB):
                    t = TPB * b + j
                    act_e.wait_ge(att_ps, t + 1)
                    act_e.activation(rows[:, t, :], ps_att[j], ACT.Copy).then_inc(att_set, 1)

            def normed(b):
                act_e.wait_ge(scale2, 2 * (b // HB) + 2)
                for t in range(TPB * b, TPB * (b + 1)):
                    a = rows[:, t, 0:D]
                    ins = act_e.activation(a, a, ACT.Identity, bias=att_bias[:, t:t + 1], scale=att_scale[:, t:t + 1])
                ins.then_inc(norm2, 1)

            copy_qT(0)
            copy_qT(1)
            act_e.wait_ge(ctxg_ps, 1)
            act_e.activation(ctx_sb[:, :, D:DE], ps_ctxg, ACT.Copy).then_inc(ctxg_set, 1)
            for b in range(2, HB + 2):
                copy_qT(b)
                if b - 2 < RAW:
                    split_high(act_e, b - 2)
            exps(0)
            copy_qT(HB + 2)
            copy_qT(HB + 3)
            copy_pT(0)
            copy_pT(1)
            copy_att(0)
            copy_pT(2)
            copy_att(1)
            copy_pT(3)
            exps(1)
            copy_att(2)
            copy_att(3)
            copy_pT(4)
            copy_pT(5)
            copy_att(4)
            normed(0)
            copy_pT(6)
            copy_att(5)
            normed(1)
            copy_pT(7)
            copy_att(6)
            normed(2)
            copy_att(7)
            for b in range(HB - 1, B):
                normed(b)
            with act_e.Fori(RAW, PIECES) as c:
                split_high(act_e, c)
            act_e.wait_ge(gshift_set, 1)
            act_e.activation(gexp[:], gshift[:], ACT.Exp).then_inc(gexp_set, 1)

            act_e.wait_ge(row_bias_set, 1)
            with act_e.Fori(0, B) as b:
                act_e.wait_ge(x1_set, b + 1)
                for j in range(TPB):
                    t = TPB * b + j
                    ins = act_e.activation(at(rows, t)[:, 0:D], at(x_sb, t), ACT.Identity, bias=one(row_bias[:, :], t),
                                           scale=one(rstd[:, 2, :], t))
                ins.then_inc(rows_set, 1)

            act_e.activation(inv_sq[:, 0:1], inv_sq[:, 0:1], ACT.Silu)
            act_e.wait_ge(tables_set, 1)

            def first_block_sent():
                act_e.wait_ge(first_sent[0], 16 * NT // GROUPS)
                groups = act_e.value_load(groups_t[0:1, 0:1], min_val=1, max_val=GROUPS)
                for g in range(1, GROUPS):
                    with act_e.If(groups > g):
                        act_e.wait_ge(first_sent[g], 16 * NT // GROUPS)

            def all_first_sent():
                for g in range(GROUPS):
                    act_e.wait_ge(first_sent[g], 16 * NT // GROUPS)

            def wait_unless_zero(of, count):
                with act_e.If(count > 0):
                    act_e.wait_ge(of, count)
                    act_e.sem_inc(rows_seen, 1)

            def load_rows(b, s):
                all_sent = act_e.value_load(rows_t[0:1, bass.ds(b, 1)], min_val=0, max_val=16 * NT)
                wait_unless_zero(last_sent, all_sent)
                if later(b, 2):
                    act_e.wait_ge(tokT_ps, b - 1)
                    act_e.wait_ge(keys_set, b - 1)
                act_e.dma_start(tok[:, s, :], at(slots_t, b)).then_inc(tok_in[s], 16)

            def tok_high(b, s):
                act_e.wait_ge(tokT_ps, b + 1)
                act_e.activation(tokT_hi[:, s], ps_tokT.rearrange("p (k c) -> p k c", k=KD), ACT.Copy).then_inc(tokT_hi_set, 1)

            def silu(b, h):
                act_e.wait_ge(gu_ps, 2 * b + h + 1)
                if later(b, 1):
                    act_e.wait_ge(act_set, 2 * b + h - 1)
                act_e.activation(gated[:, h, :], ps_g[h][:, :], ACT.Silu).then_inc(gated_set, 1)

            def act_high(b, h):
                act_e.wait_ge(aT_ps, 2 * b + h + 1)
                if later(b, 1):
                    act_e.wait_ge(down_done, 2 * b + h - 1)
                act_e.activation(aT_hi[:, h], ps_aT[h][:, :].rearrange("p (k c) -> p k c", k=CH), ACT.Copy).then_inc(aT_hi_set, 1)

            def low_result(b):
                act_e.wait_ge(down_done, 2 * b + 2)
                if later(b, 1):
                    act_e.wait_ge(y_set, b)
                act_e.activation(y_low, ps_y[:, D:2 * D], ACT.Copy, scale=at(keys, b)[:, 0:1].bitcast(F32)).then_inc(y_low_set, 1)

            def experts(b, s, ahead=2):
                silu(b, 0)
                act_high(b - 1, 1)
                if ahead > 0:
                    tok_high(b + 1, 1 - s)
                if ahead > 1:
                    load_rows(b + 3, 1 - s)
                silu(b, 1)
                act_high(b, 0)
                low_result(b - 1)
                if ahead > 0:
                    split_due(act_e, b, split_high)

            first_block_sent()
            load_rows(0, 0)
            tok_high(0, 0)
            silu(0, 0)
            all_first_sent()
            load_rows(1, 1)
            load_rows(2, 0)
            silu(0, 1)
            act_high(0, 0)
            tok_high(1, 1)
            load_rows(3, 1)
            split_due(act_e, 0, split_high)
            experts(1, 1)
            experts(2, 0)
            with act_e.Fori(1, NBLK // 2 - 2) as i:
                experts(2 * i + 1, 1)
                experts(2 * i + 2, 0)
            experts(NBLK - 4, 1)
            experts(NBLK - 3, 0, ahead=1)
            experts(NBLK - 2, 1, ahead=1)
            experts(NBLK - 1, 0, ahead=0)
            act_high(NBLK - 1, 1)
            low_result(NBLK - 1)

        @block.tensor
        def _(pe):
            pe.wait_ge(const, 8)
            pe.wait_ge(ctx_in, 16)
            for g in range(B // 2):
                if g >= 2:
                    pe.wait_ge(ctxT_set, g - 1)
                for b in range(2):
                    for k in range(KD):
                        ins = pe.transpose(ps_ctxT[g % 2][:, b, k, :], ctx_sb[:, 2 * g + b, k * P:(k + 1) * P], ident[0:T, 0:T])
                ins.then_inc(ctxT_ps, 1)

            def turn_q(b):
                pe.wait_ge(q_set, b + 1)
                if b >= 2:
                    pe.wait_ge(qT_set, b - 1)
                for j in range(TPB):
                    for k in range(KD):
                        ins = pe.transpose(ps_qT[b % 2][:, KD * j + k, :], q_sb[:, b % 2, j, k * P:(k + 1) * P], ident[:])
                ins.then_inc(qT_ps, 1)

            def logits(b):
                pe.wait_ge(qT_set, b + 1)
                if b >= 2:
                    pe.wait_ge(masked, b - 1)
                    pe.wait_ge(x_gates, b - 1)
                for j in range(TPB):
                    for k in range(KD):
                        ins = pe.matmul(ps_logit[b % 2][:, j, :], qT[:, b % 2, KD * j + k, :], ctxT[:, b, k, :],
                                        start=(k == 0), stop=(k == KD - 1))
                ins.then_inc(logit_ps, 1)

            def turn_probs(b):
                pe.wait_ge(probs_set, b // HB + 1)
                if b >= 2:
                    pe.wait_ge(pT_set, b - 1)
                for j in range(TPB):
                    ins = pe.transpose(ps_pT[b % 2][:, j, :], logit[:, TPB * b + j, :], ident[:])
                ins.then_inc(pT_ps, 1)

            def values(b):
                pe.wait_ge(pT_set, b + 1)
                for j in range(TPB):
                    t = TPB * b + j
                    if t >= 2:
                        pe.wait_ge(att_set, t - 1)
                    pe.matmul(ps_att[j], probsT[:, b % 2, j, :], ctx_sb[:, b, :], start=True, stop=True).then_inc(att_ps, 1)

            turn_q(0)
            turn_q(1)
            pe.wait_ge(ctxT_set, B // 2)
            pe.wait_ge(ctxw_set, 1)
            logits(0)
            logits(1)
            pe.wait_ge(wg_set, 2)
            for b in range(B):
                for k in range(KD):
                    ins = pe.matmul(ps_ctxg[:, b, :], ctxT[:, b, k, 0:T], wg_sb[:, k, 1, :], start=(k == 0), stop=(k == KD - 1))
            ins.then_inc(ctxg_ps, 1)
            for k in range(KD):
                ins = pe.matmul(ps_sums, ones_f[:], wg_sb[:, k, :, :].rearrange("p i e -> p (i e)"),
                                start=(k == 0), stop=(k == KD - 1))
            ins.then_inc(sums_ps, 1)
            turn_q(2)
            for b in range(2, B):
                if b + 1 < B:
                    turn_q(b + 1)
                logits(b)
                if b == HB + 1:
                    pe.wait_ge(ctxg_set, 1)
                    turn_probs(0)
                if b == HB + 2:
                    pe.wait_ge(sums_set, 1)
                    turn_probs(1)
                    values(0)
            turn_probs(2)
            values(1)
            turn_probs(3)
            values(2)
            values(3)
            turn_probs(4)
            turn_probs(5)
            values(4)
            turn_probs(6)
            values(5)
            turn_probs(7)
            values(6)
            values(7)

            pe.wait_ge(chosen_set, 1)
            picks = chosen[:].rearrange("p n e -> p (n e)")
            for t in range(NT):
                pe.matmul(ps_count, ones[:], picks[:, E * t:E * (t + 1)], start=(t == 0), stop=(t == NT - 1))
            pe.matmul(ps_rank, before[:], picks, start=True, stop=False)
            for d in range(1, NT):
                ins = pe.matmul(ps_rank[:, E * d:], ones[:], picks[:, 0:E * (NT - d)], start=False, stop=(d == NT - 1))
            ins.then_inc(rank_ps, 1)

            def turn_tok(b, s):
                pe.wait_ge(tok_in[s], arrival(b, s))
                if later(b, 1):
                    pe.wait_ge(tokT_lo_set, b)
                for k in range(KD):
                    ins = pe.transpose(ps_tokT[:, k * P:(k + 1) * P], tok[:, s, k * P:(k + 1) * P], ident[:])
                ins.then_inc(tokT_ps, 1)

            def gate_up(b, s, h, place):
                if h == 0:
                    pe.wait_ge(tokT_lo_set, b + 1)
                if later(b, 1):
                    pe.wait_ge(act_set, 2 * b + h - 1)
                for k in range(KD):
                    for tokens, part in ((tokT_hi, 0), (tokT_hi, 1), (tokT_lo, 0)):
                        for half, ps in ((0, ps_g[h]), (1, ps_u[h])):
                            w = w2[:, bass.ds(place + k * (GU // KD) + half, 1), 2 * h:2 * h + 2, part, :]
                            ins = pe.matmul(ps[:, :], tokens[:, s, k, :], w.rearrange("p a g d -> p (a g) d"),
                                            start=(k == 0 and tokens is tokT_hi and part == 0),
                                            stop=(k == KD - 1 and tokens is tokT_lo))
                ins.then_inc(gu_ps, 1)

            def turn_act(b, h):
                pe.wait_ge(act_set, 2 * b + h + 1)
                if later(b, 1):
                    pe.wait_ge(aT_lo_set, 2 * b + h - 1)
                for c in range(CH):
                    ins = pe.transpose(ps_aT[h][:, c * P:(c + 1) * P], act[:, h, c * P:(c + 1) * P], ident[:])
                ins.then_inc(aT_ps, 1)

            def down(b, h, place):
                pe.wait_ge(aT_lo_set, 2 * b + h + 1)
                if h == 0 and later(b, 1):
                    pe.wait_ge(y_set, b)
                for c in range(CH):
                    w = w2[:, bass.ds(place + GU + h, 1), c, :, :]
                    pe.matmul(ps_y[:, :], aT_hi[:, h, c, :], w.rearrange("p a t d -> p (a t d)"),
                              start=(h == 0 and c == 0), stop=False, skip_group_check=True)
                    ins = pe.matmul(ps_y[:, 0:D], aT_lo[:, h, c, :], w[:, :, 0, :].rearrange("p a d -> p (a d)"),
                                    start=False, stop=(h == 1 and c == CH - 1), skip_group_check=True)
                ins.then_inc(down_done, 1)

            def place_of(b):
                return pe.value_load(place_t[0:1, bass.ds(b, 1)], min_val=0, max_val=PIECES)

            def weights_there(b):
                pe.wait_ge(w_lo, pe.value_load(weights_t[0:1, bass.ds(b, 1)], min_val=PIECES, max_val=PIECES * E))

            def experts(b, s, last=False):
                place, place_before = place_of(b), place_of(b - 1)
                weights_there(b)
                gate_up(b, s, 0, place)
                turn_act(b - 1, 1)
                down(b - 1, 0, place_before)
                if not last:
                    turn_tok(b + 1, 1 - s)
                gate_up(b, s, 1, place)
                turn_act(b, 0)
                down(b - 1, 1, place_before)

            pe.wait_ge(tables_set, 1)
            turn_tok(0, 0)
            place = place_of(0)
            weights_there(0)
            gate_up(0, 0, 0, place)
            gate_up(0, 0, 1, place)
            turn_act(0, 0)
            turn_tok(1, 1)
            with pe.Fori(0, NBLK // 2 - 1) as i:
                experts(2 * i + 1, 1)
                experts(2 * i + 2, 0)
            experts(NBLK - 2, 1)
            experts(NBLK - 1, 0, last=True)
            turn_act(NBLK - 1, 1)
            place = place_of(NBLK - 1)
            down(NBLK - 1, 0, place)
            down(NBLK - 1, 1, place)


_INS = ["x", "ctx_1024", "mask_BxSxS2_ik1", "L0_xattn_gamma", "L0_xattn_beta", "L0_ffn_w_gate", "L0_ffn_w_gate_up",
        "L0_ffn_w_down"]


def kernel(**inputs):
    import numpy as np
    import concourse.bacc as bacc
    from concourse.bass_utils import run_bass_kernel_spmd as run

    nc = bacc.Bacc("TRN2", target_bir_lowering=False, num_devices=1)
    arrays, args = {}, []
    for name in _INS:
        a = np.ascontiguousarray(inputs[name])
        arrays[f"in_{name}"] = a
        args.append(nc.dram_tensor(f"in_{name}", a.shape, mybir.dt.from_np(a.dtype), kind="ExternalInput").ap())
    B, S, D = inputs["x"].shape
    out = nc.dram_tensor("out", (B * S + P, D), F32, kind="ExternalOutput").ap()
    build(nc, *args, out)
    result = run(nc, [arrays], core_ids=[0])
    return result.results[0]["out"][0:B * S].reshape(B, S, D)
```

```python
from contextlib import ExitStack

import concourse.bass as bass
from concourse import mybir

F32 = mybir.dt.float32
F32R = mybir.dt.float32r
BF16 = mybir.dt.bfloat16
I32 = mybir.dt.int32
ALU = mybir.AluOpType
ACT = mybir.ActivationFunctionType
X = mybir.AxisListType.X
P = 128
NEG = -9e15
NO_CAP = 3e38
EPS = 1e-5
GATE_EPS = 1e-9


def block_count(tokens, experts):
    return (2 * tokens - experts) // P + experts


def build(nc, x, ctx, mask, gamma, beta, w_gate, w_gate_up, w_down, out):
    B, S, D = x.shape
    T = ctx.shape[1]
    E, _, F2 = w_gate_up.shape
    F = F2 // 2
    KD = D // P
    TOK = B * S
    NT = TOK // P
    TPB = S // P
    HB, HT = B // 2, NT // 2
    NBLK = block_count(TOK, E)
    HALF = F // 2
    CH = HALF // P
    ROW = D + 2
    DE, TE = D + E, T + E
    PIECE = 4 * D
    PIECES = (KD * F2 + F // P * D) // PIECE
    GU = KD * F2 // PIECE
    RAW = 3
    QUOTA = 2
    OWN = 2
    GROUPS = 8
    assert NBLK % 2 == 1 and HALF == 512 and TPB == 2 and KD == 2 and F == PIECE and D == 2 * P

    x_t = x.rearrange("b (j p) d -> p (b j) d", p=P)
    mask_t = mask.rearrange("b (j p) t -> p (b j) t", p=P)
    ctx_t = ctx.rearrange("b t d -> t b d")
    out_t = out[0:TOK, :].rearrange("(n p) d -> p n d", p=P)
    slots = nc.dram_tensor("slots", (NBLK * P, ROW), F32).ap()
    slots_t = slots.rearrange("(n p) c -> p n c", p=P)

    with ExitStack() as stack:
        def sb(name, shape, dt=F32):
            return stack.enter_context(nc.sbuf_tensor(name, shape, dt))

        def sem(name):
            return stack.enter_context(nc.semaphore(name))

        ident = sb("ident", [P, P])
        before = sb("before", [P, P], BF16)
        ones = sb("ones", [P, P], BF16)
        ones_f = sb("ones_f", [P, P])
        up_to = sb("up_to", [P, E, E])
        descend = sb("descend", [P, E])
        block_start = sb("block_start", [1, NBLK])
        neg_half = sb("neg_half", [P, NT])
        gamma_b = sb("gamma_b", [P, D])
        beta_b = sb("beta_b", [P, D])
        empty = sb("empty", [P, ROW])
        x_sb = sb("x_sb", [P, NT, ROW])
        ctx_sb = sb("ctx_sb", [T, B, DE])
        w_gate_sb = sb("w_gate_sb", [P, KD, E])
        wg_sb = sb("wg_sb", [P, KD, 3, E])
        gamma_c = sb("gamma_c", [P, KD])
        beta_c = sb("beta_c", [P, KD])
        cap = sb("cap", [P, NT, T])
        ctxT = sb("ctxT", [P, B, KD, TE])
        logit = sb("logit", [P, NT, T])
        row_max = sb("row_max", [P, NT])
        row_sum = sb("row_sum", [P, NT])
        rows = sb("rows", [P, NT, DE])
        act = sb("act", [P, 2, HALF])
        gated = sb("gated", [P, 2, HALF])
        y_sb = sb("y_sb", [P, 2, D])
        q_sb = act[:, :, :].rearrange("p s (j d) -> p s j d", j=TPB)
        qT = gated[:, :, :].rearrange("p s (j c) -> p s j c", j=TPB * KD)
        probsT = y_sb[0:T, :, :].rearrange("p s (j c) -> p s j c", j=TPB)
        stats = sb("stats", [P, 3, NT, 6])
        mv = sb("mv", [P, 3, NT, 2])
        var_eps = sb("var_eps", [P, 3, NT])
        rstd = sb("rstd", [P, 3, NT])
        inv_sum = sb("inv_sum", [P, NT])
        inv_sq = sb("inv_sq", [P, NT])
        var_n = sb("var_n", [P, NT])
        att_scale = sb("att_scale", [P, NT])
        att_bias = sb("att_bias", [P, NT])
        row_bias = sb("row_bias", [P, NT])
        sums = sb("sums", [P, 2, E])
        std1 = sb("std1", [P, NT])
        x_logits = sb("x_logits", [P, NT, E])
        x1_logits = sb("x1_logits", [P, NT, E])
        gates = sb("gates", [P, NT, E])
        gmax = sb("gmax", [P, NT])
        gshift = sb("gshift", [P, NT, E])
        gexp = sb("gexp", [P, NT, E])
        gsum = sb("gsum", [P, NT])
        ginv = sb("ginv", [P, NT])
        prob = sb("prob", [P, NT, E])
        best = sb("best", [P, NT])
        tied = sb("tied", [P, NT, E])
        tied_rank = sb("tied_rank", [P, NT, E])
        first = sb("first", [P, NT])
        top1 = sb("top1", [P, NT, E])
        top2 = sb("top2", [P, NT, E])
        chosen = sb("chosen", [P, NT, E], BF16)
        denom = sb("denom", [P, NT])
        denom_g = sb("denom_g", [P, NT])
        dinv = sb("dinv", [P, NT])
        count_up = sb("count_up", [P, E], I32)
        blocks_i = sb("blocks_i", [P, E], I32)
        padded = sb("padded", [P, E])
        cum_part = sb("cum_part", [P, E, E])
        ends = sb("ends", [P, E])
        starts = sb("starts", [P, E])
        slot_c = sb("slot_c", [P, NT, E])
        last_slot = sb("last_slot", [P, NT])
        both = sb("both", [P, NT])
        lower = sb("lower", [P, NT, E])
        two_sum = sb("two_sum", [P, NT])
        low_prob = sb("low_prob", [P, NT])
        high_prob = sb("high_prob", [P, NT])
        idx = sb("idx", [P, 2, NT], I32)
        past = sb("past", [1, NBLK, E - 1])
        past_start = sb("past_start", [1, NBLK, E - 1])
        expert_f = sb("expert_f", [1, NBLK])
        expert_i = sb("expert_i", [1, NBLK], I32)
        began = sb("began", [1, NBLK])
        due = sb("due", [1, 4, NBLK])
        reached = sb("reached", [1, 2, NT])
        other = sb("other", [1, 1])
        place_t = sb("place_t", [1, NBLK], I32)
        weights_t = sb("weights_t", [1, NBLK], I32)
        rows_t = sb("rows_t", [1, NBLK], I32)
        groups_f = sb("groups_f", [1, 2])
        groups_t = sb("groups_t", [1, 2], I32)
        split_t = sb("split_t", [1, NBLK + 1], I32)
        raw = sb("raw", [P, RAW, 4, D])
        w2 = sb("w2", [P, 2 * PIECES, 4, 2, D], F32R)
        spent = ctxT[:, :, :, :].rearrange("p b k t -> p (b k t)")
        tok = spent[:, 0:2 * ROW].rearrange("p (s c) -> p s c", s=2)
        y_low = spent[:, 2 * ROW:2 * ROW + D]
        shares = spent[:, 2 * ROW + D:2 * ROW + D + 2 * NT * E].rearrange("p (i n e) -> p i n e", i=2, e=E)
        keys = logit[:, :, :].rearrange("p n t -> p (n t)")[:, 0:2 * NBLK].rearrange("p (n c) -> p n c", c=2).bitcast(I32)
        tokT_hi = sb("tokT_hi", [P, 2, KD, P], F32R)
        tokT_lo = sb("tokT_lo", [P, 2, KD, P], F32R)
        aT_hi = sb("aT_hi", [P, 2, CH, P], F32R)
        aT_lo = sb("aT_lo", [P, 2, CH, P], F32R)
        y_idx = sb("y_idx", [P, 2], I32)

        bank = [stack.enter_context(nc.psum_tensor(f"bank{i}", [P, 512], F32)) for i in range(8)]
        ps_qT = [bank[i][:, :].rearrange("p (j c) -> p j c", j=TPB * KD) for i in (0, 1)]
        ps_logit = [bank[i][:, 0:TPB * TE].rearrange("p (j t) -> p j t", j=TPB) for i in (2, 3)]
        ps_pT = [bank[i][0:T, 0:TPB * P].rearrange("p (j c) -> p j c", j=TPB) for i in (4, 5)]
        ps_att = [bank[i][:, 0:DE] for i in (6, 7)]
        ps_ctxT = [bank[i][:, 0:2 * KD * T].rearrange("p (b k t) -> p b k t", b=2, k=KD) for i in (2, 3)]
        ps_rank = bank[3][:, 0:NT * E]
        ps_count = bank[4][:, 0:E]
        ps_ctxg = bank[4][0:T, 0:B * E].rearrange("p (b e) -> p b e", e=E)
        ps_sums = bank[5][:, 0:2 * E]
        ps_colsum = bank[7][:, 0:E]
        ps_g = [bank[0], bank[2]]
        ps_u = [bank[1], bank[3]]
        ps_aT = [bank[4], bank[5]]
        ps_tokT = bank[6][:, 0:KD * P]
        ps_y = bank[7]

        def grid(ap):
            return ap.rearrange("p (n e) -> p n e", e=E)

        def over_e(ap):
            return ap.unsqueeze(2).to_broadcast([P, NT, E])

        def over_t(ap):
            return ap.unsqueeze(1).to_broadcast([P, NT, E])

        def two(buf, b):
            return buf[:, bass.ds(TPB * b, TPB), :]

        def at(buf, t):
            return buf[:, bass.ds(t, 1), :].rearrange("p a d -> p (a d)")

        def one(buf, t):
            return buf[:, bass.ds(t, 1)]

        x_in = [sem(f"x_in{i}") for i in range(4)]
        mask_in = sem("mask_in")
        ctx_in = sem("ctx_in")
        gamma_in = sem("gamma_in")
        beta_in = sem("beta_in")
        wg_in = sem("wg_in")
        raw_in = sem("raw_in")
        loading = sem("loading")
        const = sem("const")
        zeroed = sem("zeroed")
        empty_set = sem("empty_set")
        spare_out = sem("spare_out")
        slots_empty = sem("slots_empty")
        stats1 = sem("stats1")
        var1 = sem("var1")
        rstd1 = sem("rstd1")
        cols_in = sem("cols_in")
        colsum_ps = sem("colsum_ps")
        centred_set = sem("centred_set")
        wg_set = sem("wg_set")
        ctxw_set = sem("ctxw_set")
        ctxg_ps = sem("ctxg_ps")
        ctxg_set = sem("ctxg_set")
        sums_ps = sem("sums_ps")
        sums_set = sem("sums_set")
        x_gates = sem("x_gates")
        x_part = sem("x_part")
        att_part = sem("att_part")
        ids_set = sem("ids_set")
        cap_step = sem("cap_step")
        cap_set = sem("cap_set")
        xb_set = sem("xb_set")
        ctxT_ps = sem("ctxT_ps")
        ctxT_set = sem("ctxT_set")
        q_set = sem("q_set")
        qT_ps = sem("qT_ps")
        qT_set = sem("qT_set")
        logit_ps = sem("logit_ps")
        masked = sem("masked")
        max_set = sem("max_set")
        shifted = sem("shifted")
        probs_set = sem("probs_set")
        sum_set = sem("sum_set")
        inv_set = sem("inv_set")
        pT_ps = sem("pT_ps")
        pT_set = sem("pT_set")
        att_ps = sem("att_ps")
        att_set = sem("att_set")
        stats2 = sem("stats2")
        small2 = sem("small2")
        var2 = sem("var2")
        rstd2 = sem("rstd2")
        scale2 = sem("scale2")
        norm2 = sem("norm2")
        gamma_done = sem("gamma_done")
        x1_set = sem("x1_set")
        x1_own = sem("x1_own")
        x1_out = sem("x1_out")
        stats3 = sem("stats3")
        var3 = sem("var3")
        rstd3 = sem("rstd3")
        row_bias_set = sem("row_bias_set")
        rows_set = sem("rows_set")
        route = sem("route")
        tables = sem("tables")
        first_index = sem("first_index")
        last_index = sem("last_index")
        weights_set = sem("weights_set")
        rows_again = sem("rows_again")
        gshift_set = sem("gshift_set")
        gexp_set = sem("gexp_set")
        chosen_set = sem("chosen_set")
        rank_ps = sem("rank_ps")
        first_sent = [sem(f"first_sent{i}") for i in range(GROUPS)]
        last_sent = sem("last_sent")
        tables_set = sem("tables_set")
        rows_seen = sem("rows_seen")
        w_hi = sem("w_hi")
        w_lo = sem("w_lo")
        tok_in = [sem(f"tok_in{i}") for i in range(2)]
        tokT_ps = sem("tokT_ps")
        tokT_hi_set = sem("tokT_hi_set")
        tokT_lo_set = sem("tokT_lo_set")
        gu_ps = sem("gu_ps")
        gated_set = sem("gated_set")
        act_set = sem("act_set")
        aT_ps = sem("aT_ps")
        aT_hi_set = sem("aT_hi_set")
        aT_lo_set = sem("aT_lo_set")
        down_done = sem("down_done")
        y_low_set = sem("y_low_set")
        y_set = sem("y_set")
        idx_set = sem("idx_set")
        keys_set = sem("keys_set")
        adding = sem("adding")
        added = sem("added")

        def arrival(b, s):
            return 8 * (b - s) + 16

        def later(b, n):
            return not isinstance(b, int) or b >= n

        def split_high(eng, c):
            eng.wait_ge(raw_in, 16 * (c + 1))
            eng.activation(w2[:, bass.ds(c % (2 * PIECES), 1), :, 0, :].rearrange("p a g d -> p (a g) d"),
                           raw[:, bass.ds(c % RAW, 1)].rearrange("p a g d -> p (a g) d"), ACT.Copy).then_inc(w_hi, 1)

        def split_low(eng, c):
            eng.wait_ge(w_hi, c + 1)
            piece = w2[:, bass.ds(c % (2 * PIECES), 1)]
            eng.tensor_tensor(piece[:, :, :, 1, :].rearrange("p a g d -> p (a g) d"),
                              raw[:, bass.ds(c % RAW, 1)].rearrange("p a g d -> p (a g) d"),
                              piece[:, :, :, 0, :].rearrange("p a g d -> p (a g) d").bitcast(F32),
                              ALU.subtract).then_inc(w_lo, 1)

        def pieces_due(eng, b):
            lo = eng.value_load(split_t[0:1, bass.ds(b, 1)], min_val=PIECES, max_val=PIECES * E)
            hi = eng.value_load(split_t[0:1, bass.ds(b + 1, 1)], min_val=PIECES, max_val=PIECES * E)
            return lo, hi

        def split_due(eng, pieces, split):
            lo, hi = pieces
            with eng.If(lo < hi):
                with eng.Fori(lo, hi) as c:
                    split(eng, c)

        assert RAW <= HB
        block = stack.enter_context(nc.Block())

        @block.sync
        def _(sp):
            n = NT // 4
            for i in range(4):
                sp.dma_start(x_sb[:, i * n:(i + 1) * n, 0:D], x_t[:, i * n:(i + 1) * n, :]).then_inc(x_in[i], 16)
                if i == 0:
                    sp.dma_start(ctx_sb[:, :, 0:D], ctx_t).then_inc(ctx_in, 16)
                    sp.dma_start(w_gate_sb[:], w_gate.rearrange("(k p) e -> p k e", p=P)).then_inc(wg_in, 16)
                    for k in range(KD):
                        part = slice(k * P, (k + 1) * P)
                        sp.dma_start(gamma_c[:, k:k + 1], gamma[part].unsqueeze(1)).then_inc(cols_in, 16)
                        sp.dma_start(beta_c[:, k:k + 1], beta[part].unsqueeze(1)).then_inc(cols_in, 16)
                if i == 2:
                    sp.dma_start(cap[:].bitcast(I32), mask_t).then_inc(mask_in, 16)
            sp.dma_start(beta_b[:], beta.partition_broadcast(P)).then_inc(beta_in, 16)
            sp.dma_start(gamma_b[:], gamma.partition_broadcast(P)).then_inc(gamma_in, 16)

            def load_piece(e, i):
                c = PIECES * e + i
                if later(c, 1):
                    sp.wait_ge(raw_in, 16 * c)
                if not isinstance(c, int):
                    sp.sem_inc(loading, 1)
                if later(c, RAW):
                    sp.wait_ge(w_lo, c - RAW + 1)
                if not isinstance(c, int):
                    sp.sem_inc(loading, 1)
                if i < GU:
                    k, half = i // (GU // KD), i % (GU // KD)
                    sp.dma_start(raw[:, i % RAW].rearrange("p g d -> p (g d)"),
                                 w_gate_up[bass.ds(e, 1), k * P:(k + 1) * P, half * PIECE:(half + 1) * PIECE]
                                 .rearrange("a p f -> (a p) f")).then_inc(raw_in, 16)
                else:
                    f = (i - GU) * HALF
                    sp.dma_start(raw[:, i % RAW],
                                 w_down[bass.ds(e, 1), f:f + HALF, :].rearrange("a (g p) d -> p (a g) d", p=P)
                                 ).then_inc(raw_in, 16)

            for i in range(PIECES):
                load_piece(0, i)
            sp.wait_ge(empty_set, 1)
            sp.dma_start(slots_t, empty[:].unsqueeze(1).to_broadcast([P, NBLK, ROW])).then_inc(slots_empty, 16)
            sp.dma_start(out[TOK:TOK + P, :], empty[:, 0:D]).then_inc(spare_out, 16)
            with sp.Fori(0, B - OWN) as b:
                sp.wait_ge(x1_set, b + 1)
                sp.dma_start(out_t[:, bass.ds(TPB * b, TPB), :], two(x_sb, b)[:, :, 0:D]).then_inc(x1_out, 16)
            for b in range(B - OWN, B):
                sp.wait_ge(x1_own, b + 1 - (B - OWN))
                sp.dma_start(out_t[:, TPB * b:TPB * (b + 1), :], x_sb[:, TPB * b:TPB * (b + 1), 0:D]).then_inc(x1_out, 16)
            with sp.Fori(1, E) as e:
                for i in range(PIECES):
                    load_piece(e, i)

        @block.gpsimd
        def _(pool):
            pool.memset(ident[:], 0.0).then_inc(zeroed, 1)
            pool.memset(before[:], 0.0).then_inc(zeroed, 1)
            pool.memset(up_to[:], 1.0).then_inc(zeroed, 1)
            pool.memset(empty[:], 0.0).then_inc(zeroed, 1)
            pool.memset(neg_half[:], -0.5).then_inc(const, 1)
            pool.memset(ones[:], 1.0).then_inc(const, 1)
            pool.memset(ones_f[:], 1.0).then_inc(const, 1)
            pool.wait_ge(zeroed, 4)
            pool.affine_select(out=ident[:], in_=ident[:], compare_op=ALU.not_equal, fill=1.0, base=0,
                               pattern=[[-1, P]], channel_multiplier=1).then_inc(const, 1)
            pool.affine_select(out=before[:], in_=before[:], compare_op=ALU.is_ge, fill=1.0, base=0,
                               pattern=[[-1, P]], channel_multiplier=1).then_inc(const, 1)
            pool.affine_select(out=up_to[:], in_=up_to[:], compare_op=ALU.is_ge, fill=0.0, base=0,
                               pattern=[[1, E], [-1, E]], channel_multiplier=0).then_inc(const, 1)
            pool.iota(descend[:], pattern=[[-1, E]], base=E, channel_multiplier=0,
                      allow_small_or_imprecise_dtypes=True).then_inc(const, 1)
            pool.iota(block_start[:], pattern=[[P, NBLK]], base=0, channel_multiplier=0,
                      allow_small_or_imprecise_dtypes=True).then_inc(const, 1)
            pool.iota(empty[:, D + 1:D + 2].bitcast(I32), pattern=[[0, 1]], base=TOK, channel_multiplier=1).then_inc(empty_set, 1)

            def rsqrt(n, t0, t1, ready, count, done):
                pool.wait_ge(ready, count)
                pool.tensor_tensor(rstd[:, n, t0:t1], var_eps[:, n, t0:t1], neg_half[:, 0:t1 - t0], ALU.pow).then_inc(done, 1)

            pool.wait_ge(const, 8)
            rsqrt(0, 0, NT // 4, var1, 1, rstd1)
            pool.wait_ge(centred_set, 1)
            pool.tensor_copy(ctxT[:, :, :, T:TE], wg_sb[:, :, 0, :].unsqueeze(1).to_broadcast([P, B, KD, E])).then_inc(ctxw_set, 1)
            pool.wait_ge(cols_in, 32 * KD)
            for i, col in ((1, gamma_c), (2, beta_c)):
                pool.tensor_tensor(wg_sb[:, :, i, :], wg_sb[:, :, 0, :], col[:].unsqueeze(2).to_broadcast([P, KD, E]),
                                   ALU.mult).then_inc(wg_set, 1)
            for i in range(1, 4):
                rsqrt(0, i * NT // 4, (i + 1) * NT // 4, var1, i + 1, rstd1)

            def add_beta(b):
                pool.wait_ge(q_set, b + 1)
                pool.tensor_tensor(two(x_sb, b)[:, :, 0:D], two(x_sb, b)[:, :, 0:D], beta_b[:].unsqueeze(1).to_broadcast([P, TPB, D]),
                                   ALU.add).then_inc(xb_set, 1)

            def times_gamma(b):
                pool.wait_ge(norm2, b + 1)
                a = two(rows, b)[:, :, 0:D]
                pool.tensor_tensor(a, a, gamma_b[:].unsqueeze(1).to_broadcast([P, TPB, D]), ALU.mult).then_inc(gamma_done, 1)

            pool.wait_ge(beta_in, 16)
            with pool.Fori(0, RAW) as i:
                split_low(pool, i)
                add_beta(i)
            for b in range(RAW, B):
                add_beta(b)
            pool.wait_ge(gamma_in, 16)
            rsqrt(1, 0, HT, var2, 1, rstd2)
            for b in range(2):
                times_gamma(b)
            rsqrt(1, HT, NT, var2, 2, rstd2)
            for b in range(2, B):
                times_gamma(b)
            for b in range(B - OWN, B):
                pool.wait_ge(gamma_done, b + 1)
                pool.tensor_tensor(two(x_sb, b)[:, :, 0:D], two(rows, b)[:, :, 0:D], two(x_sb, b)[:, :, 0:D],
                                   ALU.add).then_inc(x1_own, 1)
            rsqrt(2, 0, HT, var3, 1, rstd3)
            pool.wait_ge(att_part, 1)
            for buf in (rows, x_sb):
                pool.iota(buf[:, :, D + 1:D + 2].bitcast(I32), pattern=[[P, NT], [0, 1]], base=0,
                          channel_multiplier=1).then_inc(ids_set, 1)
            rsqrt(2, HT, NT, var3, 2, rstd3)

            def send(buf, half, n, done):
                pool.indirect_dma_start(
                    out=slots, out_offset=bass.IndirectOffsetOnAxis(ap=idx[:, half, n:n + 1], axis=0),
                    in_=buf[:, n, 0:ROW], in_offset=None).then_inc(done, 16)

            pool.wait_ge(slots_empty, 16)
            pool.wait_ge(ids_set, 2)
            pool.wait_ge(first_index, 1)
            pool.wait_ge(weights_set, 1)
            for n in range(NT):
                if n % TPB == 0:
                    pool.wait_ge(rows_set, n // TPB + 1)
                send(rows, 0, n, first_sent[n * GROUPS // NT])
            pool.wait_ge(last_index, 1)
            pool.wait_ge(weights_set, 2)
            for n in range(NT):
                if n % TPB == 0:
                    pool.wait_ge(rows_again, n // TPB + 1)
                send(x_sb, 1, n, last_sent)
            pool.wait_ge(x1_out, 16 * B)
            pool.wait_ge(spare_out, 16)

            def add(b, s):
                pool.wait_ge(y_set, b + 1)
                pool.wait_ge(idx_set, b + 1)
                pool.sem_inc(adding, 1)
                pool.indirect_dma_start(
                    out=out, out_offset=bass.IndirectOffsetOnAxis(ap=y_idx[:, s:s + 1], axis=0),
                    in_=y_sb[:, s, :], in_offset=None, compute_op=ALU.add).then_inc(added, 16)
                pool.wait_ge(added, 16 * (b + 1))

            add(0, 0)
            with pool.Fori(0, NBLK // 2) as i:
                add(2 * i + 1, 1)
                add(2 * i + 2, 0)

        @block.vector
        def _(dve):
            ready2 = (HT, 3 * HT)

            done = {route: 0, tables: 0}

            def after(chain):
                dve.wait_ge(chain, done[chain])

            def step(chain, ins):
                ins.then_inc(chain, 1)
                done[chain] += 1

            def aggregate(n, t0, t1, done, count):
                dve.wait_ge(done, count)
                for t in range(t0, t1):
                    dve.bn_aggr(mv[:, n, t, :], stats[:, n, t, :]).then_inc(done, 1)
                dve.wait_ge(done, count + t1 - t0)

            def x_stats(i):
                n = NT // 4
                dve.wait_ge(x_in[i], 16)
                for t in range(i * n, (i + 1) * n):
                    dve.bn_stats(stats[:, 0, t, :], x_sb[:, t, 0:D]).then_inc(stats1, 1)
                aggregate(0, i * n, (i + 1) * n, stats1, (2 * i + 1) * n)
                dve.tensor_scalar(var_eps[:, 0, i * n:(i + 1) * n], mv[:, 0, i * n:(i + 1) * n, 1], EPS, None,
                                  ALU.add).then_inc(var1, 1)

            def queries(b):
                dve.wait_ge(rstd1, b * 4 // B + 1)
                if b >= 2:
                    dve.wait_ge(qT_ps, b - 1)
                for j in range(TPB):
                    t = TPB * b + j
                    ins = dve.tensor_scalar(q_sb[:, b % 2, j, :], x_sb[:, t, 0:D], mv[:, 0, t, 0:1], rstd[:, 0, t:t + 1],
                                            ALU.subtract, ALU.mult)
                ins.then_inc(q_set, 1)

            def masked_logits(b):
                dve.wait_ge(logit_ps, b + 1)
                tiles = slice(TPB * b, TPB * (b + 1))
                dve.scalar_tensor_tensor(out=logit[:, tiles, :], in0=ps_logit[b % 2][:, :, 0:T], scalar=float(D) ** -0.5,
                                         in1=cap[:, tiles, :], op0=ALU.mult, op1=ALU.min).then_inc(masked, 1)
                dve.tensor_copy(x_logits[:, tiles, :], ps_logit[b % 2][:, :, T:TE]).then_inc(x_gates, 1)

            def shift(h):
                part, top = logit[:, h * HT:(h + 1) * HT, :], row_max[:, h * HT:(h + 1) * HT]
                dve.wait_ge(masked, (h + 1) * HB)
                dve.tensor_reduce(top, part, X, ALU.max).then_inc(max_set, 1)
                dve.wait_ge(max_set, h + 1)
                dve.tensor_tensor(part, part, top.unsqueeze(2).to_broadcast([P, HT, T]), ALU.subtract).then_inc(shifted, 1)

            def divisors(h):
                part = slice(h * HT, (h + 1) * HT)
                dve.wait_ge(probs_set, h + 1)
                dve.tensor_reduce(row_sum[:, part], logit[:, part, :], X, ALU.add).then_inc(sum_set, 1)
                dve.wait_ge(sum_set, h + 1)
                dve.reciprocal(inv_sum[:, part], row_sum[:, part]).then_inc(inv_set, 1)
                dve.wait_ge(inv_set, 2 * h + 1)
                dve.tensor_tensor(inv_sq[:, part], inv_sum[:, part], inv_sum[:, part], ALU.mult).then_inc(inv_set, 1)

            def att_stats(b):
                for t in range(TPB * b, TPB * (b + 1)):
                    dve.wait_ge(att_set, t + 1)
                    dve.bn_stats(stats[:, 1, t, :], rows[:, t, 0:D]).then_inc(stats2, 1)

            def variances(h):
                aggregate(1, h * HT, (h + 1) * HT, stats2, ready2[h])
                part = slice(h * HT, (h + 1) * HT)
                dve.wait_ge(inv_set, 2 * h + 2)
                dve.tensor_tensor(var_n[:, part], mv[:, 1, part, 1], inv_sq[:, part], ALU.mult).then_inc(small2, 1)
                dve.wait_ge(small2, 1 + h)
                dve.tensor_scalar(var_eps[:, 1, part], var_n[:, part], EPS, None, ALU.add).then_inc(var2, 1)

            def scales(h):
                part = slice(h * HT, (h + 1) * HT)
                dve.wait_ge(rstd2, h + 1)
                dve.tensor_tensor(att_scale[:, part], inv_sum[:, part], rstd[:, 1, part], ALU.mult).then_inc(scale2, 1)
                dve.wait_ge(scale2, 2 * h + 1)
                dve.scalar_tensor_tensor(out=att_bias[:, part], in0=mv[:, 1, part, 0], scalar=-1.0, in1=att_scale[:, part],
                                         op0=ALU.mult, op1=ALU.mult).then_inc(scale2, 1)

            def residual(b):
                dve.wait_ge(gamma_done, b + 1)
                dve.wait_ge(xb_set, b + 1)
                tiles = slice(TPB * b, TPB * (b + 1))
                dve.tensor_tensor(x_sb[:, tiles, 0:D], rows[:, tiles, 0:D], x_sb[:, tiles, 0:D], ALU.add).then_inc(x1_set, 1)

            def x1_stats(b):
                if b < B - OWN:
                    dve.wait_ge(x1_set, b + 1)
                else:
                    dve.wait_ge(x1_own, b + 1 - (B - OWN))
                for t in range(TPB * b, TPB * (b + 1)):
                    dve.bn_stats(stats[:, 2, t, :], x_sb[:, t, 0:D]).then_inc(stats3, 1)

            def x1_variances(h):
                part = slice(h * HT, (h + 1) * HT)
                aggregate(2, h * HT, (h + 1) * HT, stats3, (HT, 3 * HT)[h])
                dve.tensor_scalar(var_eps[:, 2, part], mv[:, 2, part, 1], EPS, None, ALU.add).then_inc(var3, 1)

            def row_biases(h):
                part = slice(h * HT, (h + 1) * HT)
                dve.wait_ge(rstd3, h + 1)
                dve.scalar_tensor_tensor(out=row_bias[:, part], in0=mv[:, 2, part, 0], scalar=-1.0, in1=rstd[:, 2, part],
                                         op0=ALU.mult, op1=ALU.mult).then_inc(row_bias_set, 1)

            def x_share():
                dve.reciprocal(std1[:], rstd[:, 0, :]).then_inc(x_part, 1)
                dve.wait_ge(x_gates, B)
                dve.wait_ge(x_part, 1)
                dve.tensor_tensor(x_logits[:], x_logits[:], over_e(std1[:]), ALU.mult).then_inc(x_part, 1)
                dve.wait_ge(sums_set, 1)
                dve.wait_ge(x_part, 2)
                dve.tensor_tensor(x_logits[:], x_logits[:], over_t(sums[:, 1, :]), ALU.add).then_inc(x_part, 1)

            def x1_share():
                dve.wait_ge(scale2, 4)
                dve.tensor_tensor(shares[:, 0], rows[:, :, D:DE], over_e(att_scale[:]), ALU.mult).then_inc(att_part, 1)
                dve.tensor_tensor(shares[:, 1], over_e(att_bias[:]), over_t(sums[:, 0, :]), ALU.mult).then_inc(x_part, 1)
                dve.wait_ge(x_part, 4)
                dve.wait_ge(att_part, 1)
                dve.tensor_tensor(shares[:, 0], shares[:, 0], x_logits[:], ALU.add).then_inc(x_part, 1)
                dve.wait_ge(x_part, 5)
                dve.tensor_tensor(x1_logits[:], shares[:, 0], shares[:, 1], ALU.add).then_inc(x_part, 1)
                dve.wait_ge(x_part, 6)

            x_stats(0)
            queries(0)
            queries(1)
            dve.wait_ge(colsum_ps, 1)
            dve.scalar_tensor_tensor(out=wg_sb[:, :, 0, :], in0=ps_colsum.unsqueeze(1).to_broadcast([P, KD, E]), scalar=-1.0 / D,
                                     in1=w_gate_sb[:], op0=ALU.mult, op1=ALU.add).then_inc(centred_set, 1)
            x_stats(1)
            x_stats(2)
            queries(2)
            dve.wait_ge(mask_in, 16)
            dve.tensor_scalar(cap[:], cap[:].bitcast(I32), 0.0, NO_CAP, ALU.not_equal, ALU.mult).then_inc(cap_step, 1)
            dve.wait_ge(cap_step, 1)
            dve.tensor_scalar(cap[:], cap[:], NEG, None, ALU.add).then_inc(cap_set, 1)
            dve.wait_ge(cap_set, 1)
            queries(3)
            masked_logits(0)
            x_stats(3)
            for b in range(1, HB):
                queries(b + 3)
                masked_logits(b)
            dve.wait_ge(sums_ps, 1)
            dve.tensor_copy(sums[:].rearrange("p i e -> p (i e)"), ps_sums).then_inc(sums_set, 1)
            shift(0)
            queries(HB + 3)
            for b in range(HB, B - 2):
                masked_logits(b)
            divisors(0)
            masked_logits(B - 2)
            att_stats(0)
            masked_logits(B - 1)
            shift(1)
            x_share()
            for b in range(1, HB):
                att_stats(b)
            variances(0)
            divisors(1)
            att_stats(HB)
            scales(0)
            for b in range(HB + 1, B):
                att_stats(b)
            variances(1)
            residual(0)
            residual(1)
            x1_stats(0)
            x1_stats(1)
            scales(1)
            x1_share()

            step(route, dve.tensor_reduce(gmax[:], x1_logits[:], X, ALU.max))
            residual(2)
            after(route)
            step(route, dve.tensor_tensor(gshift[:], x1_logits[:], over_e(gmax[:]), ALU.subtract))
            after(route)
            step(route, dve.scalar_tensor_tensor(out=tied_rank[:], in0=gshift[:], scalar=0.0, in1=over_t(descend[:]),
                                                 op0=ALU.is_equal, op1=ALU.mult))
            residual(HB - 1)
            after(route)
            step(route, dve.tensor_reduce(first[:], tied_rank[:], X, ALU.max))
            x1_stats(2)
            after(route)
            step(route, dve.tensor_tensor(top1[:], tied_rank[:], over_e(first[:]), ALU.is_equal))
            x1_stats(HB - 1)
            x1_variances(0)
            after(route)
            step(route, dve.scalar_tensor_tensor(out=gates[:], in0=top1[:], scalar=-NO_CAP, in1=gshift[:], op0=ALU.mult, op1=ALU.add))
            residual(HB)
            after(route)
            step(route, dve.tensor_reduce(best[:], gates[:], X, ALU.max))
            x1_stats(HB)
            after(route)
            step(route, dve.tensor_tensor(tied[:], gates[:], over_e(best[:]), ALU.is_equal))
            residual(HB + 1)
            after(route)
            step(route, dve.tensor_tensor(tied_rank[:], tied[:], over_t(descend[:]), ALU.mult))
            x1_stats(HB + 1)
            after(route)
            step(route, dve.tensor_reduce(first[:], tied_rank[:], X, ALU.max))
            after(route)
            step(route, dve.tensor_tensor(top2[:], tied_rank[:], over_e(first[:]), ALU.is_equal))
            x1_stats(HB + 2)
            after(route)
            dve.tensor_tensor(chosen[:], top1[:], top2[:], ALU.add).then_inc(chosen_set, 1)
            row_biases(0)
            dve.wait_ge(chosen_set, 1)
            step(route, dve.tensor_tensor(tied_rank[:], chosen[:], over_t(descend[:]), ALU.mult))
            after(route)
            step(route, dve.tensor_reduce(first[:], tied_rank[:], X, ALU.max))
            x1_stats(B - 1)
            x1_variances(1)
            after(route)
            step(tables, dve.tensor_tensor(lower[:], tied_rank[:], over_e(first[:]), ALU.is_equal))

            dve.wait_ge(rank_ps, 1)
            step(route, dve.tensor_scalar(count_up[:], ps_count, float(P - 1), None, ALU.add))
            after(route)
            step(route, dve.tensor_scalar(blocks_i[:], count_up[:], P.bit_length() - 1, None, ALU.arith_shift_right))
            after(route)
            step(route, dve.tensor_scalar(padded[:], blocks_i[:], float(P), float(P), ALU.mult, ALU.max))
            after(route)
            step(route, dve.tensor_tensor(cum_part[:], up_to[:], padded[:].unsqueeze(1).to_broadcast([P, E, E]), ALU.mult))
            after(route)
            step(route, dve.tensor_reduce(ends[:], cum_part[:], X, ALU.add))
            after(route)
            step(route, dve.tensor_tensor(starts[:], ends[:], padded[:], ALU.subtract))
            after(route)
            step(route, dve.scalar_tensor_tensor(out=slot_c[:], in0=grid(ps_rank), scalar=1.0, in1=over_t(starts[:]),
                                                 op0=ALU.add, op1=ALU.add))
            after(route)
            step(route, dve.tensor_tensor(slot_c[:], slot_c[:], chosen[:], ALU.mult))
            dve.wait_ge(rstd3, 2)
            dve.tensor_tensor(gshift[:], gshift[:], over_e(rstd[:, 2, :]), ALU.mult).then_inc(gshift_set, 1)
            row_biases(1)
            after(route)
            step(route, dve.tensor_reduce(last_slot[:], slot_c[:], X, ALU.max))
            step(route, dve.tensor_reduce(both[:], slot_c[:], X, ALU.add))
            after(route)
            dve.scalar_tensor_tensor(out=idx[:, 0, :], in0=both[:], scalar=-1.0, in1=last_slot[:],
                                     op0=ALU.add, op1=ALU.subtract).then_inc(first_index, 1)
            dve.tensor_scalar(idx[:, 1, :], last_slot[:], -1.0, None, ALU.add).then_inc(last_index, 1)

            dve.wait_ge(gexp_set, 1)
            after(tables)
            step(tables, dve.tensor_reduce(gsum[:], gexp[:], X, ALU.add))
            step(tables, dve.tensor_tensor(prob[:], gexp[:], chosen[:], ALU.mult))
            after(tables)
            step(tables, dve.reciprocal(ginv[:], gsum[:]))
            step(tables, dve.tensor_reduce(two_sum[:], prob[:], X, ALU.add))
            step(tables, dve.tensor_tensor(gates[:], prob[:], lower[:], ALU.mult))
            after(tables)
            step(tables, dve.tensor_tensor(denom[:], two_sum[:], ginv[:], ALU.mult))
            step(tables, dve.tensor_reduce(low_prob[:], gates[:], X, ALU.add))
            after(tables)
            step(tables, dve.scalar_tensor_tensor(out=denom_g[:], in0=denom[:], scalar=GATE_EPS, in1=gsum[:],
                                                  op0=ALU.max, op1=ALU.mult))
            step(tables, dve.tensor_tensor(high_prob[:], two_sum[:], low_prob[:], ALU.subtract))
            after(tables)
            step(tables, dve.reciprocal(dinv[:], denom_g[:]))
            after(tables)
            dve.wait_ge(ids_set, 1)
            dve.tensor_tensor(rows[:, :, D], low_prob[:], dinv[:], ALU.mult).then_inc(weights_set, 1)
            dve.wait_ge(ids_set, 2)
            dve.tensor_tensor(x_sb[:, :, D], high_prob[:], dinv[:], ALU.mult).then_inc(weights_set, 1)

            ends_row = ends[0:1, 0:E - 1].unsqueeze(1).to_broadcast([1, NBLK, E - 1])
            start_row = block_start[:].unsqueeze(2).to_broadcast([1, NBLK, E - 1])
            step(route, dve.tensor_tensor(past[:], start_row, ends_row, ALU.is_ge))
            after(route)
            step(route, dve.tensor_reduce(expert_f[:], past[:], X, ALU.add))
            step(tables, dve.tensor_tensor(past_start[:], past[:], ends_row, ALU.mult))
            after(route)
            step(route, dve.tensor_copy(expert_i[:], expert_f[:]))
            after(tables)
            step(tables, dve.tensor_reduce(began[:], past_start[:], X, ALU.max))
            after(route)
            step(route, dve.tensor_scalar(expert_i[:], expert_i[:], 1, None, ALU.bitwise_and))
            after(tables)
            step(tables, dve.tensor_tensor(due[:, 0, :], block_start[:], began[:], ALU.subtract))
            after(route)
            step(route, dve.tensor_scalar(place_t[:], expert_i[:], float(PIECES), None, ALU.mult))
            after(tables)
            step(tables, dve.tensor_scalar(due[:, 0, :], due[:, 0, :], QUOTA / P, float(QUOTA + PIECES), ALU.mult, ALU.add))
            step(route, dve.tensor_scalar(weights_t[:], expert_f[:], float(PIECES), float(PIECES), ALU.mult, ALU.add))
            step(route, dve.tensor_scalar(rows_t[:], expert_f[:], 1.0, 16.0 * NT, ALU.min, ALU.mult))
            step(route, dve.tensor_scalar(due[:, 1, :], expert_f[:], float(PIECES), None, ALU.mult))
            for b in range(2):
                step(route, dve.tensor_scalar(reached[:, b, :], grid(ps_rank)[0:1, :, 0], float(P * (b + 1)), None, ALU.is_lt))
            step(route, dve.tensor_scalar(other[:], expert_f[:, 1:2], 1.0, float(GROUPS), ALU.min, ALU.mult))
            after(route)
            after(tables)
            step(tables, dve.tensor_tensor(due[:, 0, :], due[:, 0, :], due[:, 1, :], ALU.add))
            step(route, dve.tensor_scalar(due[:, 2, :], due[:, 1, :], 2.0 * PIECES, float(PIECES * E), ALU.add, ALU.min))
            step(route, dve.tensor_scalar(due[:, 3, :], due[:, 1, :], float(PIECES), None, ALU.add))
            step(route, dve.tensor_reduce(groups_f[:], reached[:].rearrange("p b (g n) -> p b g n", g=GROUPS)[:, :, :, 0], X, ALU.add))
            after(route)
            after(tables)
            step(tables, dve.tensor_tensor(due[:, 0, 0:NBLK - 1], due[:, 0, 0:NBLK - 1], due[:, 3, 1:NBLK], ALU.max))
            step(route, dve.tensor_copy(groups_t[:, 0:1], groups_f[:, 0:1]))
            step(route, dve.tensor_tensor(groups_t[:, 1:2], groups_f[:, 1:2], other[:], ALU.max))
            after(tables)
            step(tables, dve.tensor_tensor(split_t[:, 1:NBLK + 1], due[:, 0, :], due[:, 2, :], ALU.min))
            after(tables)
            after(route)
            dve.memset(split_t[:, 0:1], PIECES).then_inc(tables_set, 1)
            with dve.Fori(RAW, PIECES) as c:
                split_low(dve, c)

            def copy_rows(b):
                tiles = slice(TPB * b, TPB * (b + 1))
                dve.wait_ge(x1_out, 16 * B)
                dve.wait_ge(rows_set, b + 1)
                dve.tensor_copy(x_sb[:, tiles, 0:D], rows[:, tiles, 0:D]).then_inc(rows_again, 1)

            def take_keys(b, s):
                dve.wait_ge(tok_in[s], arrival(b, s))
                dve.tensor_copy(at(keys, b), tok[:, s, D:D + 2].bitcast(I32)).then_inc(keys_set, 1)

            def tok_low(b, s):
                dve.wait_ge(tokT_hi_set, b + 1)
                dve.tensor_tensor(tokT_lo[:, s], ps_tokT.rearrange("p (k c) -> p k c", k=KD), tokT_hi[:, s].bitcast(F32),
                                  ALU.subtract).then_inc(tokT_lo_set, 1)

            def gate_half(b, h):
                dve.wait_ge(gated_set, 2 * b + h + 1)
                if later(b, 1):
                    dve.wait_ge(aT_ps, 2 * b + h - 1)
                dve.tensor_tensor(act[:, h, :], gated[:, h, :], ps_u[h][:, :], ALU.mult).then_inc(act_set, 1)

            def act_low(b, h):
                dve.wait_ge(aT_hi_set, 2 * b + h + 1)
                dve.tensor_tensor(aT_lo[:, h], ps_aT[h][:, :].rearrange("p (k c) -> p k c", k=CH), aT_hi[:, h].bitcast(F32),
                                  ALU.subtract).then_inc(aT_lo_set, 1)

            def weighted(b, s):
                if later(b, 2):
                    dve.wait_ge(added, 16 * (b - 1))
                dve.wait_ge(keys_set, b + 1)
                dve.tensor_copy(y_idx[:, s:s + 1], at(keys, b)[:, 1:2]).then_inc(idx_set, 1)
                dve.wait_ge(y_low_set, b + 1)
                dve.scalar_tensor_tensor(out=y_sb[:, s, :], in0=ps_y[:, 0:D], scalar=at(keys, b)[:, 0:1].bitcast(F32),
                                         in1=y_low, op0=ALU.mult, op1=ALU.add).then_inc(y_set, 1)

            def experts(b, s, last=False):
                gate_half(b, 0)
                act_low(b - 1, 1)
                if not last:
                    take_keys(b + 1, 1 - s)
                    tok_low(b + 1, 1 - s)
                    pieces = pieces_due(dve, b)
                gate_half(b, 1)
                act_low(b, 0)
                weighted(b - 1, 1 - s)
                if not last:
                    split_due(dve, pieces, split_low)

            for b in range(HB):
                copy_rows(b)
            take_keys(0, 0)
            tok_low(0, 0)
            for b in range(HB, B):
                copy_rows(b)
            gate_half(0, 0)
            take_keys(1, 1)
            tok_low(1, 1)
            gate_half(0, 1)
            act_low(0, 0)
            split_due(dve, pieces_due(dve, 0), split_low)
            experts(1, 1)
            experts(2, 0)
            with dve.Fori(1, NBLK // 2 - 1) as i:
                experts(2 * i + 1, 1)
                experts(2 * i + 2, 0)
            experts(NBLK - 2, 1)
            experts(NBLK - 1, 0, last=True)
            act_low(NBLK - 1, 1)
            weighted(NBLK - 1, 0)

        @block.scalar
        def _(act_e):
            for g in range(B // 2):
                act_e.wait_ge(ctxT_ps, g + 1)
                act_e.activation(ctxT[:, 2 * g:2 * g + 2, :, 0:T], ps_ctxT[g % 2], ACT.Copy).then_inc(ctxT_set, 1)

            def copy_qT(b):
                act_e.wait_ge(qT_ps, b + 1)
                if b >= 2:
                    act_e.wait_ge(logit_ps, b - 1)
                act_e.activation(qT[:, b % 2], ps_qT[b % 2], ACT.Copy).then_inc(qT_set, 1)

            def exps(h):
                act_e.wait_ge(shifted, h + 1)
                part = logit[:, h * HT:(h + 1) * HT, :]
                act_e.activation(part, part, ACT.Exp).then_inc(probs_set, 1)

            def copy_pT(b):
                act_e.wait_ge(pT_ps, b + 1)
                act_e.activation(probsT[:, b % 2], ps_pT[b % 2], ACT.Copy).then_inc(pT_set, 1)

            def copy_att(b):
                for j in range(TPB):
                    t = TPB * b + j
                    act_e.wait_ge(att_ps, t + 1)
                    act_e.activation(rows[:, t, :], ps_att[j], ACT.Copy).then_inc(att_set, 1)

            def normed(b):
                act_e.wait_ge(scale2, 2 * (b // HB) + 2)
                for t in range(TPB * b, TPB * (b + 1)):
                    a = rows[:, t, 0:D]
                    ins = act_e.activation(a, a, ACT.Identity, bias=att_bias[:, t:t + 1], scale=att_scale[:, t:t + 1])
                ins.then_inc(norm2, 1)

            copy_qT(0)
            copy_qT(1)
            act_e.wait_ge(ctxg_ps, 1)
            act_e.activation(ctx_sb[:, :, D:DE], ps_ctxg, ACT.Copy).then_inc(ctxg_set, 1)
            for b in range(2, HB + 2):
                copy_qT(b)
                if b - 2 < RAW:
                    split_high(act_e, b - 2)
            exps(0)
            copy_qT(HB + 2)
            copy_qT(HB + 3)
            copy_pT(0)
            copy_pT(1)
            copy_att(0)
            copy_pT(2)
            copy_att(1)
            copy_pT(3)
            exps(1)
            copy_att(2)
            copy_att(3)
            copy_pT(4)
            copy_pT(5)
            copy_att(4)
            copy_pT(6)
            copy_att(5)
            copy_pT(7)
            copy_att(6)
            normed(0)
            copy_att(7)
            for b in range(1, B):
                normed(b)
            with act_e.Fori(RAW, PIECES) as c:
                split_high(act_e, c)

            def slot_rows(b):
                for t in range(TPB * b, TPB * (b + 1)):
                    ins = act_e.activation(rows[:, t, 0:D], x_sb[:, t, 0:D], ACT.Identity, bias=row_bias[:, t:t + 1],
                                           scale=rstd[:, 2, t:t + 1])
                ins.then_inc(rows_set, 1)

            act_e.wait_ge(row_bias_set, 1)
            for b in range(HB):
                slot_rows(b)
            act_e.wait_ge(gshift_set, 1)
            act_e.activation(gexp[:], gshift[:], ACT.Exp).then_inc(gexp_set, 1)
            act_e.wait_ge(row_bias_set, 2)
            for b in range(HB, B):
                slot_rows(b)
            act_e.activation(inv_sq[:, 0:1], inv_sq[:, 0:1], ACT.Silu)
            act_e.wait_ge(tables_set, 1)

            def early_block_sent(b):
                act_e.wait_ge(first_sent[0], 16 * NT // GROUPS)
                groups = act_e.value_load(groups_t[0:1, b:b + 1], min_val=1, max_val=GROUPS)
                for g in range(1, GROUPS):
                    with act_e.If(groups > g):
                        act_e.wait_ge(first_sent[g], 16 * NT // GROUPS)

            def all_first_sent():
                for g in range(GROUPS):
                    act_e.wait_ge(first_sent[g], 16 * NT // GROUPS)

            def wait_unless_zero(of, count):
                with act_e.If(count > 0):
                    act_e.wait_ge(of, count)
                    act_e.sem_inc(rows_seen, 1)

            def load_rows(b, s):
                all_sent = act_e.value_load(rows_t[0:1, bass.ds(b, 1)], min_val=0, max_val=16 * NT)
                wait_unless_zero(last_sent, all_sent)
                if later(b, 2):
                    act_e.wait_ge(tokT_ps, b - 1)
                    act_e.wait_ge(keys_set, b - 1)
                act_e.dma_start(tok[:, s, :], at(slots_t, b)).then_inc(tok_in[s], 16)

            def tok_high(b, s):
                act_e.wait_ge(tokT_ps, b + 1)
                act_e.activation(tokT_hi[:, s], ps_tokT.rearrange("p (k c) -> p k c", k=KD), ACT.Copy).then_inc(tokT_hi_set, 1)

            def silu(b, h):
                act_e.wait_ge(gu_ps, 2 * b + h + 1)
                if later(b, 1):
                    act_e.wait_ge(act_set, 2 * b + h - 1)
                act_e.activation(gated[:, h, :], ps_g[h][:, :], ACT.Silu).then_inc(gated_set, 1)

            def act_high(b, h):
                act_e.wait_ge(aT_ps, 2 * b + h + 1)
                if later(b, 1):
                    act_e.wait_ge(down_done, 2 * b + h - 1)
                act_e.activation(aT_hi[:, h], ps_aT[h][:, :].rearrange("p (k c) -> p k c", k=CH), ACT.Copy).then_inc(aT_hi_set, 1)

            def low_result(b):
                act_e.wait_ge(down_done, 2 * b + 2)
                if later(b, 1):
                    act_e.wait_ge(y_set, b)
                act_e.activation(y_low, ps_y[:, D:2 * D], ACT.Copy, scale=at(keys, b)[:, 0:1].bitcast(F32)).then_inc(y_low_set, 1)

            def experts(b, s, loads=1, late=False, last=False):
                silu(b, 0)
                act_high(b - 1, 1)
                if not last:
                    if loads > 1:
                        load_rows(b + 2, s)
                    tok_high(b + 1, 1 - s)
                    if loads > 0:
                        load_rows(b + 3, 1 - s)
                    pieces = pieces_due(act_e, b)
                silu(b, 1)
                act_high(b, 0)
                low_result(b - 1)
                if late:
                    load_rows(b + 2, s)
                if not last:
                    split_due(act_e, pieces, split_high)

            early_block_sent(0)
            load_rows(0, 0)
            tok_high(0, 0)
            early_block_sent(1)
            load_rows(1, 1)
            silu(0, 0)
            tok_high(1, 1)
            silu(0, 1)
            act_high(0, 0)
            all_first_sent()
            load_rows(2, 0)
            split_due(act_e, pieces_due(act_e, 0), split_high)
            experts(1, 1, loads=0, late=True)
            experts(2, 0, loads=2)
            with act_e.Fori(1, NBLK // 2 - 2) as i:
                experts(2 * i + 1, 1)
                experts(2 * i + 2, 0)
            experts(NBLK - 4, 1)
            for b in range(NBLK - 3, NBLK):
                experts(b, b % 2, loads=0, last=b == NBLK - 1)
            act_high(NBLK - 1, 1)
            low_result(NBLK - 1)

        @block.tensor
        def _(pe):
            pe.wait_ge(const, 8)
            pe.wait_ge(ctx_in, 16)
            for g in range(B // 2):
                if g >= 2:
                    pe.wait_ge(ctxT_set, g - 1)
                for b in range(2):
                    for k in range(KD):
                        ins = pe.transpose(ps_ctxT[g % 2][:, b, k, :], ctx_sb[:, 2 * g + b, k * P:(k + 1) * P], ident[0:T, 0:T])
                ins.then_inc(ctxT_ps, 1)

            def turn_q(b):
                pe.wait_ge(q_set, b + 1)
                if b >= 2:
                    pe.wait_ge(qT_set, b - 1)
                for j in range(TPB):
                    for k in range(KD):
                        ins = pe.transpose(ps_qT[b % 2][:, KD * j + k, :], q_sb[:, b % 2, j, k * P:(k + 1) * P], ident[:])
                ins.then_inc(qT_ps, 1)

            def logits(b):
                pe.wait_ge(qT_set, b + 1)
                if b >= 2:
                    pe.wait_ge(masked, b - 1)
                    pe.wait_ge(x_gates, b - 1)
                for j in range(TPB):
                    for k in range(KD):
                        ins = pe.matmul(ps_logit[b % 2][:, j, :], qT[:, b % 2, KD * j + k, :], ctxT[:, b, k, :],
                                        start=(k == 0), stop=(k == KD - 1))
                ins.then_inc(logit_ps, 1)

            def turn_probs(b):
                pe.wait_ge(probs_set, b // HB + 1)
                if b >= 2:
                    pe.wait_ge(pT_set, b - 1)
                for j in range(TPB):
                    ins = pe.transpose(ps_pT[b % 2][:, j, :], logit[:, TPB * b + j, :], ident[:])
                ins.then_inc(pT_ps, 1)

            def values(b):
                pe.wait_ge(pT_set, b + 1)
                for j in range(TPB):
                    t = TPB * b + j
                    if t >= 2:
                        pe.wait_ge(att_set, t - 1)
                    pe.matmul(ps_att[j], probsT[:, b % 2, j, :], ctx_sb[:, b, :], start=True, stop=True).then_inc(att_ps, 1)

            pe.wait_ge(wg_in, 16)
            for k in range(KD):
                ins = pe.matmul(ps_colsum, ones_f[:], w_gate_sb[:, k, :], start=(k == 0), stop=(k == KD - 1))
            ins.then_inc(colsum_ps, 1)
            turn_q(0)
            turn_q(1)
            pe.wait_ge(ctxT_set, B // 2)
            pe.wait_ge(ctxw_set, 1)
            logits(0)
            logits(1)
            pe.wait_ge(wg_set, 2)
            for b in range(B):
                for k in range(KD):
                    ins = pe.matmul(ps_ctxg[:, b, :], ctxT[:, b, k, 0:T], wg_sb[:, k, 1, :], start=(k == 0), stop=(k == KD - 1))
            ins.then_inc(ctxg_ps, 1)
            for k in range(KD):
                ins = pe.matmul(ps_sums, ones_f[:], wg_sb[:, k, 1:3, :].rearrange("p i e -> p (i e)"),
                                start=(k == 0), stop=(k == KD - 1))
            ins.then_inc(sums_ps, 1)
            turn_q(2)
            for b in range(2, B):
                if b + 1 < B:
                    turn_q(b + 1)
                logits(b)
                if b == HB + 1:
                    pe.wait_ge(ctxg_set, 1)
                    turn_probs(0)
                if b == HB + 2:
                    pe.wait_ge(sums_set, 1)
                    turn_probs(1)
                    values(0)
            turn_probs(2)
            values(1)
            turn_probs(3)
            values(2)
            values(3)
            turn_probs(4)
            turn_probs(5)
            values(4)
            turn_probs(6)
            values(5)
            turn_probs(7)
            values(6)
            values(7)

            pe.wait_ge(chosen_set, 1)
            picks = chosen[:].rearrange("p n e -> p (n e)")
            for t in range(NT):
                pe.matmul(ps_count, ones[:], picks[:, E * t:E * (t + 1)], start=(t == 0), stop=(t == NT - 1))
            pe.matmul(ps_rank, before[:], picks, start=True, stop=False)
            for d in range(1, NT):
                ins = pe.matmul(ps_rank[:, E * d:], ones[:], picks[:, 0:E * (NT - d)], start=False, stop=(d == NT - 1))
            ins.then_inc(rank_ps, 1)

            def turn_tok(b, s):
                pe.wait_ge(tok_in[s], arrival(b, s))
                if later(b, 1):
                    pe.wait_ge(tokT_lo_set, b)
                for k in range(KD):
                    ins = pe.transpose(ps_tokT[:, k * P:(k + 1) * P], tok[:, s, k * P:(k + 1) * P], ident[:])
                ins.then_inc(tokT_ps, 1)

            def gate_up(b, s, h, place):
                if h == 0:
                    pe.wait_ge(tokT_lo_set, b + 1)
                if later(b, 1):
                    pe.wait_ge(act_set, 2 * b + h - 1)
                for k in range(KD):
                    for tokens, part in ((tokT_hi, 0), (tokT_hi, 1), (tokT_lo, 0)):
                        for half, ps in ((0, ps_g[h]), (1, ps_u[h])):
                            w = w2[:, bass.ds(place + k * (GU // KD) + half, 1), 2 * h:2 * h + 2, part, :]
                            ins = pe.matmul(ps[:, :], tokens[:, s, k, :], w.rearrange("p a g d -> p (a g) d"),
                                            start=(k == 0 and tokens is tokT_hi and part == 0),
                                            stop=(k == KD - 1 and tokens is tokT_lo))
                ins.then_inc(gu_ps, 1)

            def turn_act(b, h):
                pe.wait_ge(act_set, 2 * b + h + 1)
                if later(b, 1):
                    pe.wait_ge(aT_lo_set, 2 * b + h - 1)
                for c in range(CH):
                    ins = pe.transpose(ps_aT[h][:, c * P:(c + 1) * P], act[:, h, c * P:(c + 1) * P], ident[:])
                ins.then_inc(aT_ps, 1)

            def down(b, h, place):
                pe.wait_ge(aT_lo_set, 2 * b + h + 1)
                if h == 0 and later(b, 1):
                    pe.wait_ge(y_set, b)
                for c in range(CH):
                    w = w2[:, bass.ds(place + GU + h, 1), c, :, :]
                    pe.matmul(ps_y[:, :], aT_hi[:, h, c, :], w.rearrange("p a t d -> p (a t d)"),
                              start=(h == 0 and c == 0), stop=False, skip_group_check=True)
                    ins = pe.matmul(ps_y[:, 0:D], aT_lo[:, h, c, :], w[:, :, 0, :].rearrange("p a d -> p (a d)"),
                                    start=False, stop=(h == 1 and c == CH - 1), skip_group_check=True)
                ins.then_inc(down_done, 1)

            def place_of(b):
                return pe.value_load(place_t[0:1, bass.ds(b, 1)], min_val=0, max_val=PIECES)

            def weights_there(b):
                pe.wait_ge(w_lo, pe.value_load(weights_t[0:1, bass.ds(b, 1)], min_val=PIECES, max_val=PIECES * E))

            def experts(b, s, place_before=None, last=False):
                place = place_of(b)
                weights_there(b)
                gate_up(b, s, 0, place)
                if place_before is None:
                    place_before = place_of(b - 1)
                turn_act(b - 1, 1)
                down(b - 1, 0, place_before)
                if not last:
                    turn_tok(b + 1, 1 - s)
                gate_up(b, s, 1, place)
                turn_act(b, 0)
                down(b - 1, 1, place_before)
                return place

            pe.wait_ge(tables_set, 1)
            turn_tok(0, 0)
            place = place_of(0)
            weights_there(0)
            gate_up(0, 0, 0, place)
            gate_up(0, 0, 1, place)
            turn_tok(1, 1)
            turn_act(0, 0)
            place = experts(1, 1)
            experts(2, 0, place)
            with pe.Fori(1, NBLK // 2 - 1) as i:
                place = experts(2 * i + 1, 1)
                experts(2 * i + 2, 0, place)
            place = experts(NBLK - 2, 1)
            place = experts(NBLK - 1, 0, place, last=True)
            turn_act(NBLK - 1, 1)
            down(NBLK - 1, 0, place)
            down(NBLK - 1, 1, place)


_INS = ["x", "ctx_1024", "mask_BxSxS2_ik1", "L0_xattn_gamma", "L0_xattn_beta", "L0_ffn_w_gate", "L0_ffn_w_gate_up",
        "L0_ffn_w_down"]


def kernel(**inputs):
    import numpy as np
    import concourse.bacc as bacc
    from concourse.bass_utils import run_bass_kernel_spmd as run

    nc = bacc.Bacc("TRN2", target_bir_lowering=False, num_devices=1)
    arrays, args = {}, []
    for name in _INS:
        a = np.ascontiguousarray(inputs[name])
        arrays[f"in_{name}"] = a
        args.append(nc.dram_tensor(f"in_{name}", a.shape, mybir.dt.from_np(a.dtype), kind="ExternalInput").ap())
    B, S, D = inputs["x"].shape
    out = nc.dram_tensor("out", (B * S + P, D), F32, kind="ExternalOutput").ap()
    build(nc, *args, out)
    result = run(nc, [arrays], core_ids=[0])
    return result.results[0]["out"][0:B * S].reshape(B, S, D)
```
